# Optimizing a Trainium2 kernel written in Bass

```python
import numpy as np
import jax
import jax.numpy as jnp

def _softmax(x, axis=-1):
    return jax.nn.softmax(x, axis=axis)

def _gelu(x):
    return jax.nn.gelu(x, approximate=True)

def _silu(x):
    return jax.nn.silu(x)

def _sigmoid(x):
    return jax.nn.sigmoid(x)

def _layernorm(x, axis=-1, eps=1e-05):
    m = jnp.mean(x, axis=axis, keepdims=True)
    v = jnp.var(x, axis=axis, keepdims=True)
    return (x - m) / jnp.sqrt(v + eps)

def _scatter_add(tgt, idx, src, axis=0):
    return tgt.at[idx].add(src)

def _segment_sum(src, seg, n):
    return jax.ops.segment_sum(src, seg, n)
kernel_name = 'mk_conv_seq_d2_conv_nhwc384_r4_8acd6d'

def setup_inputs(seed: int=0):
    np.random.seed(seed)
    _w = jnp.asarray

    def _rec_inputs():
        import jax
        import jax.numpy as jnp
        _gk = jax.random.key(seed)
        x = -0.0002221 + 1 * jax.random.normal(jax.random.fold_in(_gk, 1), (16, 16, 16, 96), jnp.float32)
        return x
    x = _rec_inputs()

    def _L0_conv_setup():
        import jax, jax.numpy as jnp
        import numpy as np
        DECAY = 0.6
        GAIN = 0.4

        def _layernorm(x, g, b, eps=1e-05):
            m = x.mean(-1, keepdims=True)
            v = x.var(-1, keepdims=True)
            return (x - m) * jax.lax.rsqrt(v + eps) * g + b

        def _ema_scan(x, axis, reverse=False):
            a = jnp.full_like(x, DECAY)
            b = GAIN * x

            def comb(c1, c2):
                a1, b1 = c1
                a2, b2 = c2
                return (a1 * a2, a2 * b1 + b2)
            _, y = jax.lax.associative_scan(comb, (a, b), axis=axis, reverse=reverse)
            return y
        key = jax.random.key(seed)
        B, H, W, D = (16, 16, 16, 96)
        inner = 2 * D
        hidden = 4 * D
        ks = jax.random.split(key, 12)
        s = 0.02
        return {'x': jax.random.normal(ks[0], (B, H, W, D), jnp.float32), 'n1_g': jnp.ones((D,), jnp.float32), 'n1_b': jnp.zeros((D,), jnp.float32), 'w_in': s * jax.random.normal(ks[1], (D, inner), jnp.float32), 'b_in': jnp.zeros((inner,), jnp.float32), 'k_conv': s * jax.random.normal(ks[2], (3, 3, 1, inner), jnp.float32), 'on_g': jnp.ones((inner,), jnp.float32), 'on_b': jnp.zeros((inner,), jnp.float32), 'w_out': s * jax.random.normal(ks[3], (inner, D), jnp.float32), 'b_out': jnp.zeros((D,), jnp.float32), 'n2_g': jnp.ones((D,), jnp.float32), 'n2_b': jnp.zeros((D,), jnp.float32), 'w1': s * jax.random.normal(ks[4], (D, hidden), jnp.float32), 'b1': jnp.zeros((hidden,), jnp.float32), 'w2': s * jax.random.normal(ks[5], (hidden, D), jnp.float32), 'b2': jnp.zeros((D,), jnp.float32)}
    _L0_conv_all = _L0_conv_setup()
    _L0_conv_in = {k: v for k, v in _L0_conv_all.items() if k in ('n1_g', 'n1_b', 'w_in', 'b_in', 'k_conv', 'on_g', 'on_b', 'w_out', 'b_out', 'n2_g', 'n2_b', 'w1', 'b1', 'w2', 'b2')}
    del _L0_conv_all

    def _L1_conv_setup():
        import jax, jax.numpy as jnp
        import numpy as np
        B, H, W, C, T = (16, 32, 32, 96, 8)
        HID = int(4.0 * C)
        EPS = 1e-06

        def _ln(x, scale, bias):
            mu = jnp.mean(x, axis=-1, keepdims=True)
            var = jnp.mean(jnp.square(x - mu), axis=-1, keepdims=True)
            return (x - mu) * jax.lax.rsqrt(var + EPS) * scale + bias
        key = jax.random.key(seed)
        ks = jax.random.split(key, 8)
        w = lambda k, shape: jax.random.normal(k, shape, jnp.float32) * 0.02
        return {'x': jax.random.normal(ks[0], (B, H, W, C), jnp.float32), 'norm1_scale': jnp.ones((C,), jnp.float32), 'norm1_bias': jnp.zeros((C,), jnp.float32), 'Wu': w(ks[1], (C, C)), 'bu': jnp.zeros((C,), jnp.float32), 'Wg': w(ks[2], (C, C)), 'bg': jnp.zeros((C,), jnp.float32), 'A': w(ks[3], (C, C)), 'norm2_scale': jnp.ones((C,), jnp.float32), 'norm2_bias': jnp.zeros((C,), jnp.float32), 'mlp_w1': w(ks[4], (C, HID)), 'mlp_b1': jnp.zeros((HID,), jnp.float32), 'mlp_w2': w(ks[5], (HID, C)), 'mlp_b2': jnp.zeros((C,), jnp.float32)}
    _L1_conv_all = _L1_conv_setup()
    _L1_conv_in = {k: v for k, v in _L1_conv_all.items() if k in ('norm1_scale', 'norm1_bias', 'Wu', 'bu', 'Wg', 'bg', 'A', 'norm2_scale', 'norm2_bias', 'mlp_w1', 'mlp_b1', 'mlp_w2', 'mlp_b2')}
    del _L1_conv_all
    return {'x': x, 'L0_conv_n1_g': _L0_conv_in['n1_g'], 'L0_conv_n1_b': _L0_conv_in['n1_b'], 'L0_conv_w_in': _L0_conv_in['w_in'], 'L0_conv_b_in': _L0_conv_in['b_in'], 'L0_conv_k_conv': _L0_conv_in['k_conv'], 'L0_conv_on_g': _L0_conv_in['on_g'], 'L0_conv_on_b': _L0_conv_in['on_b'], 'L0_conv_w_out': _L0_conv_in['w_out'], 'L0_conv_b_out': _L0_conv_in['b_out'], 'L0_conv_n2_g': _L0_conv_in['n2_g'], 'L0_conv_n2_b': _L0_conv_in['n2_b'], 'L0_conv_w1': _L0_conv_in['w1'], 'L0_conv_b1': _L0_conv_in['b1'], 'L0_conv_w2': _L0_conv_in['w2'], 'L0_conv_b2': _L0_conv_in['b2'], 'L1_conv_norm1_scale': _L1_conv_in['norm1_scale'], 'L1_conv_norm1_bias': _L1_conv_in['norm1_bias'], 'L1_conv_Wu': _L1_conv_in['Wu'], 'L1_conv_bu': _L1_conv_in['bu'], 'L1_conv_Wg': _L1_conv_in['Wg'], 'L1_conv_bg': _L1_conv_in['bg'], 'L1_conv_A': _L1_conv_in['A'], 'L1_conv_norm2_scale': _L1_conv_in['norm2_scale'], 'L1_conv_norm2_bias': _L1_conv_in['norm2_bias'], 'L1_conv_mlp_w1': _L1_conv_in['mlp_w1'], 'L1_conv_mlp_b1': _L1_conv_in['mlp_b1'], 'L1_conv_mlp_w2': _L1_conv_in['mlp_w2'], 'L1_conv_mlp_b2': _L1_conv_in['mlp_b2']}

def reference(x, L0_conv_n1_g, L0_conv_n1_b, L0_conv_w_in, L0_conv_b_in, L0_conv_k_conv, L0_conv_on_g, L0_conv_on_b, L0_conv_w_out, L0_conv_b_out, L0_conv_n2_g, L0_conv_n2_b, L0_conv_w1, L0_conv_b1, L0_conv_w2, L0_conv_b2, L1_conv_norm1_scale, L1_conv_norm1_bias, L1_conv_Wu, L1_conv_bu, L1_conv_Wg, L1_conv_bg, L1_conv_A, L1_conv_norm2_scale, L1_conv_norm2_bias, L1_conv_mlp_w1, L1_conv_mlp_b1, L1_conv_mlp_w2, L1_conv_mlp_b2):
    import jax
    import jax.numpy as jnp

    def _L0_conv_ref(x, n1_g, n1_b, w_in, b_in, k_conv, on_g, on_b, w_out, b_out, n2_g, n2_b, w1, b1, w2, b2):
        import jax, jax.numpy as jnp
        import numpy as np
        DECAY = 0.6
        GAIN = 0.4

        def _layernorm(x, g, b, eps=1e-05):
            m = x.mean(-1, keepdims=True)
            v = x.var(-1, keepdims=True)
            return (x - m) * jax.lax.rsqrt(v + eps) * g + b

        def _ema_scan(x, axis, reverse=False):
            a = jnp.full_like(x, DECAY)
            b = GAIN * x

            def comb(c1, c2):
                a1, b1 = c1
                a2, b2 = c2
                return (a1 * a2, a2 * b1 + b2)
            _, y = jax.lax.associative_scan(comb, (a, b), axis=axis, reverse=reverse)
            return y
        inner = w_in.shape[1]
        h = _layernorm(x, n1_g, n1_b)
        p = h @ w_in + b_in
        local = jax.lax.conv_general_dilated(p, k_conv, window_strides=(1, 1), padding='SAME', dimension_numbers=('NHWC', 'HWIO', 'NHWC'), feature_group_count=inner)
        lr = _ema_scan(local, axis=2)
        rl = _ema_scan(local, axis=2, reverse=True)
        tb = _ema_scan(local, axis=1)
        bt = _ema_scan(local, axis=1, reverse=True)
        mixed = 0.25 * (lr + rl + tb + bt) + local
        mixed = _layernorm(mixed, on_g, on_b)
        x = x + (mixed @ w_out + b_out)
        h2 = _layernorm(x, n2_g, n2_b)
        m = jax.nn.gelu(h2 @ w1 + b1, approximate=False) @ w2 + b2
        return x + m

    def _L1_conv_ref(x, norm1_scale, norm1_bias, Wu, bu, Wg, bg, A, norm2_scale, norm2_bias, mlp_w1, mlp_b1, mlp_w2, mlp_b2):
        import jax, jax.numpy as jnp
        import numpy as np
        B, H, W, C, T = (16, 32, 32, 96, 8)
        HID = int(4.0 * C)
        EPS = 1e-06

        def _ln(x, scale, bias):
            mu = jnp.mean(x, axis=-1, keepdims=True)
            var = jnp.mean(jnp.square(x - mu), axis=-1, keepdims=True)
            return (x - mu) * jax.lax.rsqrt(var + EPS) * scale + bias
        xn = _ln(x, norm1_scale, norm1_bias)
        u = jnp.einsum('bhwc,cd->bhwd', xn, Wu) + bu
        g = jax.nn.sigmoid(jnp.einsum('bhwc,cd->bhwd', xn, Wg) + bg)

        def step(h, _):
            h = g * jnp.einsum('bhwc,cd->bhwd', h, A) + (1.0 - g) * u
            return (h, None)
        h_last, _ = jax.lax.scan(step, jnp.zeros_like(u), None, length=T)
        x = x + h_last
        xn2 = _ln(x, norm2_scale, norm2_bias)
        m = jax.nn.gelu(jnp.einsum('bhwc,cf->bhwf', xn2, mlp_w1) + mlp_b1)
        m = jnp.einsum('bhwf,fc->bhwc', m, mlp_w2) + mlp_b2
        return x + m

    def _gn(v, G=32, eps=1e-05):
        B_, H_, W_, C_ = v.shape
        g = v.reshape(B_, H_, W_, G, C_ // G)
        m = jnp.mean(g, axis=(1, 2, 4), keepdims=True)
        s = jnp.var(g, axis=(1, 2, 4), keepdims=True)
        return ((g - m) / jnp.sqrt(s + eps)).reshape(v.shape)

    def _ln_c(v, eps=1e-06):
        m = jnp.mean(v, axis=-1, keepdims=True)
        s = jnp.var(v, axis=-1, keepdims=True)
        return (v - m) / jnp.sqrt(s + eps)

    def _ln_t(v, eps=1e-05):
        m = jnp.mean(v, axis=-1, keepdims=True)
        s = jnp.var(v, axis=-1, keepdims=True)
        return (v - m) / jnp.sqrt(s + eps)

    def _to_tokens(v):
        B_, H_, W_, C_ = v.shape
        return v.reshape(B_, H_ * W_, C_)

    def _from_tokens(t, like):
        return t.reshape(like.shape)
    x = _L0_conv_ref(x, L0_conv_n1_g, L0_conv_n1_b, L0_conv_w_in, L0_conv_b_in, L0_conv_k_conv, L0_conv_on_g, L0_conv_on_b, L0_conv_w_out, L0_conv_b_out, L0_conv_n2_g, L0_conv_n2_b, L0_conv_w1, L0_conv_b1, L0_conv_w2, L0_conv_b2)
    x = _L1_conv_ref(x, L1_conv_norm1_scale, L1_conv_norm1_bias, L1_conv_Wu, L1_conv_bu, L1_conv_Wg, L1_conv_bg, L1_conv_A, L1_conv_norm2_scale, L1_conv_norm2_bias, L1_conv_mlp_w1, L1_conv_mlp_b1, L1_conv_mlp_w2, L1_conv_mlp_b2)
    return x

_drawn_inputs = setup_inputs


def setup_inputs(seed=0):
    import zlib

    import numpy as np

    out = dict(_drawn_inputs(seed))
    spreads = {'L0_conv_n1_g': (1.0, 0.2),
     'L0_conv_n1_b': (0.0, 0.1),
     'L0_conv_b_in': (0.0, 0.1),
     'L0_conv_on_g': (1.0, 0.2),
     'L0_conv_on_b': (0.0, 0.298),
     'L0_conv_b_out': (0.0, 0.1),
     'L0_conv_n2_g': (1.0, 0.6),
     'L0_conv_n2_b': (0.0, 0.8),
     'L0_conv_b1': (0.0, 0.439),
     'L0_conv_b2': (0.0, 0.1),
     'L1_conv_norm1_scale': (1.0, 0.6),
     'L1_conv_norm1_bias': (0.0, 0.8),
     'L1_conv_bu': (0.0, 0.1),
     'L1_conv_bg': (0.0, 0.8),
     'L1_conv_norm2_scale': (1.0, 0.6),
     'L1_conv_norm2_bias': (0.0, 0.8),
     'L1_conv_mlp_b1': (0.0, 0.384),
     'L1_conv_mlp_b2': (0.0, 0.1)}
    factors = {'L1_conv_Wg': 5.197, 'L1_conv_A': 4.928}
    for name, (base, spread) in spreads.items():
        noise = np.random.default_rng([zlib.crc32(name.encode()), seed]).standard_normal(out[name].shape)
        drawn = base * np.exp(spread * noise) if base else spread * noise
        out[name] = jnp.asarray(drawn.astype(out[name].dtype))
    for name, factor in factors.items():
        out[name] = (out[name] * factor).astype(out[name].dtype)
    return out
```

```python
from contextlib import ExitStack

import concourse.bass as bass
from concourse import mybir

F32 = mybir.dt.float32
F32R = mybir.dt.float32r
ALU = mybir.AluOpType
ACT = mybir.ActivationFunctionType

IMAGES, SIDE, D = 16, 16, 96
INNER, HIDDEN, STEPS = 2 * D, 4 * D, 8
DECAY, GAIN = 0.6, 0.4
P = 128
TOKENS = SIDE * SIDE
TILES = IMAGES // 2
TILE = 2 * TOKENS
CHUNKS = TILE // P
HB = INNER - P
HJ = HIDDEN // P
ROW = SIDE + 1
IMG = ROW * ROW
LEAD = ROW + 1
TAPS = [(dy, dx) for dy in (-1, 0, 1) for dx in (-1, 0, 1)]
EPS0, EPS1 = 1e-5, 1e-6

COLS = (["n1_g", "n1_b", "b_inA", "b_inB"] + [f"kA{t}" for t in range(9)] + [f"kB{t}" for t in range(9)]
        + ["on_gA", "on_gB", "on_bA", "on_bB", "n2_g", "n2_b", "b1_0", "b1_1", "b1_2",
           "s3", "c3", "bu", "bg", "s4", "c4", "m1_0", "m1_1", "m1_2"])
W0 = {"w_in": (0, 384), "w_outA": (384, 480), "w_outB": (480, 576), "w1": (576, 960), "w2": (960, 1248)}
W1 = {"Wu": (0, 96), "Wg": (96, 192), "A": (192, 288), "m1": (288, 672), "m2": (672, 960)}


def tile_known(t):
    return not isinstance(t, int) or 0 <= t < TILES


def wait(engine, sem, count):
    if not isinstance(count, int) or count > 0:
        engine.wait_ge(sem, count)


def build(nc, x, cols_d, rows_d, w0_d, w1_d, mix_d, ident_d, out):
    x_d = x.rearrange("(t i p) f -> t p i f", i=2, p=P)
    out_d = out.rearrange("(t i p) f -> t p i f", i=2, p=P)

    with ExitStack() as ctx:
        def sb(name, cols, dt=F32, rows=P):
            return ctx.enter_context(nc.sbuf_tensor(name, [rows, cols], dt))

        def sem(name):
            return ctx.enter_context(nc.semaphore(name))

        bank = [ctx.enter_context(nc.psum_tensor(f"bank{b}", [P, 512], F32)) for b in range(8)]

        cols = sb("cols", len(COLS))
        rows = sb("rows", 3 * D)
        w0 = sb("w0", 1248)
        w1 = sb("w1", 960)
        mix = sb("mix", 2 * TOKENS)
        ident = sb("ident", P)
        ones = sb("ones", P)
        onbA, onbB = sb("onbA", P), sb("onbB", P)
        wi_f, w1_f, m1_f, w3_f = sb("wi_f", 384), sb("w1_f", 384), sb("m1_f", 384), sb("w3_f", 288)
        wi_h, w1_h, m1_h, w3_h = (sb(n, c, F32R) for n, c in (("wi_h", 384), ("w1_h", 384), ("m1_h", 384), ("w3_h", 288)))
        wi_l, w1_l, m1_l, w3_l = (sb(n, c, F32R) for n, c in (("wi_l", 384), ("w1_l", 384), ("m1_l", 384), ("w3_l", 288)))
        woA_f, woB_f = sb("woA_f", D), sb("woB_f", D)
        woA, woB0, woB1 = sb("woA", D), sb("woB0", D), sb("woB1", D)
        a_i, a_half, wuT = sb("a_i", D), sb("a_half", D), sb("wuT", D)
        bias = sb("bias", 16)
        brow = sb("brow", D)
        B = {n: bias[:, k:k + 1] for k, n in enumerate(
            ["inA", "inB", "b1_0", "b1_1", "b1_2", "m1_0", "m1_1", "m1_2", "u", "u_neg_half", "g_half", "v_half"])}

        def col(name, n=P):
            k = COLS.index(name)
            return cols[0:n, k:k + 1]

        x_all = sb("x_all", TILES * CHUNKS * D)
        st1, mv1, rs1, ng1 = sb("st1", 24), sb("mv1", 8), sb("rs1", 4), sb("ng1", 4)
        st2, mv2, rs2, ng2 = sb("st2", 24), sb("mv2", 8), sb("rs2", 4), sb("ng2", 4)
        stm, mvm, rsm = sb("stm", 24), sb("mvm", 8), sb("rsm", 4)
        st3, mv3, rs3 = sb("st3", 24), sb("mv3", 8), sb("rs3", 4)
        st4, mv4, rs4, ng4 = sb("st4", 24), sb("mv4", 8), sb("rs4", 4), sb("ng4", 4)
        power, minus, eps0, eps1 = (sb(n, 4) for n in ("power", "minus", "eps0", "eps1"))
        xn1, xn2, xn3, xn4 = (sb(f"xn{k}", CHUNKS * D) for k in (1, 2, 3, 4))
        xc1, xc2, xc3, xc4 = (sb(f"xc{k}", TILE) for k in (1, 2, 3, 4))
        xh1, xh2, xh3, xh4 = (sb(f"xh{k}", TILE, F32R) for k in (1, 2, 3, 4))
        xl1, xl2, xl3, xl4 = (sb(f"xl{k}", TILE, F32R) for k in (1, 2, 3, 4))
        SPAN_A, SPAN_B = LEAD + 2 * IMG + LEAD, LEAD + IMG + LEAD
        pA, pB = sb("pA", SPAN_A), sb("pB", SPAN_B)
        cA, cB = sb("cA", (2 * SIDE + 1) * SIDE), sb("cB", TOKENS)
        local = sb("local", 2 * 2 * INNER)
        mixed = sb("mixed", 2 * 2 * INNER)
        mcA, mcB = sb("mcA", TILE), sb("mcB", TOKENS)
        xb, x2, x2b = sb("xb", CHUNKS * D), sb("x2", CHUNKS * D), sb("x2b", CHUNKS * D)
        hid = sb("hid", HJ * TILE)
        th, nu, vh, q, h8 = (sb(n, TILE) for n in ("th", "nu", "vh", "q", "h8"))
        x4, x4b, y = sb("x4", CHUNKS * D), sb("x4b", CHUNKS * D), sb("y", CHUNKS * D)
        hid1 = sb("hid1", HJ * TILE)

        s = {n: sem(n) for n in (
            "w0_loaded", "w1_loaded", "ones_set", "pads_zero", "prep", "prep_psum",
            "x_loaded", "bn1_step", "mv1_ready", "ln1_step", "xn1_ready", "trx_done", "x1_split", "x1_lo",
            "p_psum", "p_ready", "conv_step", "ltr_done", "local_ready", "mix_done", "mixed_ready",
            "bnm_step", "mvm_ready", "lnm_step", "mtr_done", "mc_ready", "wout_done", "xb_ready", "x2_ready",
            "bn2_step", "mv2_ready", "ln2_step", "xn2_ready", "x2b_ready", "tr2_done", "x2_split", "x2_lo",
            "hid_psum", "gelu_done", "w2_done", "x3_ready",
            "bn3_step", "mv3_ready", "ln3_step", "xn3_ready", "tr3_done", "x3_split", "x3_lo", "ugv_psum",
            "ugv_ready", "bits_set", "seeded", "step_done", "q_ready", "h8_ready", "trh_done", "x4_ready",
            "bn4_step", "mv4_ready", "ln4_step", "xn4_ready", "x4b_ready", "tr4_done", "x4_split", "x4_lo",
            "hid1_psum", "gelu1_done", "m2_done", "y_ready", "y_stored")}

        block = ctx.enter_context(nc.Block())

        def x_tile(t):
            return x_all[:, bass.ts(t, CHUNKS * D)]

        def run(engine, body, first, steady, after, last):
            for i in range(first, steady):
                body(i)
            with engine.Fori(steady, after) as i:
                body(i)
            for i in range(after, last):
                body(i)

        def run0(engine, body):
            run(engine, body, -2, 2, TILES - 2, TILES + 2)

        def run1(engine, body):
            run(engine, body, -2, 2, TILES - 2, TILES + 2)

        @block.sync
        def _(sp):
            sp.dma_start(x_tile(0).rearrange("p (i f) -> p i f", i=2), x_d[0]).then_inc(s["x_loaded"], 16)
            sp.dma_start(cols[:, :], cols_d).then_inc(s["w0_loaded"], 16)
            sp.dma_start(ident[:, :], ident_d).then_inc(s["w0_loaded"], 16)
            sp.dma_start(w0[:, :], w0_d).then_inc(s["w0_loaded"], 16)
            sp.dma_start(rows[:, :], rows_d.broadcast_to([P, 3 * D])).then_inc(s["w0_loaded"], 16)
            sp.dma_start(mix[:, :].rearrange("p (k n) -> p k n", k=2),
                         mix_d.rearrange("(k p) n -> p k n", p=P)).then_inc(s["w0_loaded"], 16)
            sp.dma_start(w1[:, :], w1_d).then_inc(s["w1_loaded"], 16)
            for t in range(1, TILES):
                sp.wait_ge(s["x_loaded"], 16 * t)
                sp.dma_start(x_tile(t).rearrange("p (i f) -> p i f", i=2), x_d[t]).then_inc(s["x_loaded"], 16)
            with sp.Fori(0, TILES) as t:
                sp.wait_ge(s["y_ready"], t + 1)
                sp.dma_start(out_d[bass.ds(t, 1)].rearrange("t p i f -> (t p) i f"),
                             y[:, :].rearrange("p (i f) -> p i f", i=2)).then_inc(s["y_stored"], 16)
            sp.wait_ge(s["y_stored"], 16 * TILES)

        @block.gpsimd
        def _(pool):
            pool.memset(ones[:, :], 1.0).then_inc(s["ones_set"], 1)
            for constant, value in ((power, -0.5), (minus, -1.0), (eps0, EPS0), (eps1, EPS1)):
                pool.memset(constant[:, :], value).then_inc(s["ones_set"], 1)
            for zeroed in (pA, pB, woB0, woB1):
                pool.memset(zeroed[:, :], 0.0).then_inc(s["pads_zero"], 1)
            pool.wait_ge(s["ones_set"], 5)

            def split_low(lo, v, hi):
                return pool.tensor_tensor(lo[0:D, :], v[0:D, :], hi[0:D, :].bitcast(F32), ALU.subtract)

            def inverse_std(rs, mv, eps, step, done):
                pool.tensor_tensor(rs[:, :], mv[:, 1:8:2], eps[:, :], ALU.add).then_inc(step, 1)
                pool.wait_ge(step, done + 1)
                pool.tensor_tensor(rs[:, :], rs[:, :], power[:, :], ALU.pow).then_inc(step, 1)

            def minus_mean(ng, mv, step):
                pool.tensor_tensor(ng[:, :], mv[:, 0:8:2], minus[:, :], ALU.mult).then_inc(step, 1)

            def normalize(xn, v, ng, rs, ready):
                for k in range(CHUNKS):
                    pool.tensor_scalar(xn[:, k * D:(k + 1) * D], v[:, k * D:(k + 1) * D], ng[:, k:k + 1],
                                       rs[:, k:k + 1], ALU.add, ALU.mult).then_inc(ready, 1)

            def add_row(res, v, row, ready):
                pool.tensor_tensor(res[:, :].rearrange("p (k c) -> p k c", c=D),
                                   v.rearrange("p (k c) -> p k c", c=D),
                                   row.unsqueeze(1).broadcast_to([P, CHUNKS, D]), ALU.add).then_inc(ready, 1)

            def body0(i):
                n, f, m, g = i + 2, i + 1, i - 1, i - 2
                if tile_known(n):
                    pool.wait_ge(s["mv1_ready"], 4 * n + 4)
                    wait(pool, s["xn1_ready"], 4 * n)
                    minus_mean(ng1, mv1, s["ln1_step"])
                    inverse_std(rs1, mv1, eps0, s["ln1_step"], 4 * n + 1)
                    pool.wait_ge(s["ln1_step"], 4 * n + 3)
                    pool.tensor_tensor(ng1[:, :], ng1[:, :], rs1[:, :], ALU.mult).then_inc(s["ln1_step"], 1)
                if tile_known(f):
                    pool.wait_ge(s["x1_split"], 2 * f + 2)
                    wait(pool, s["p_psum"], 2 * f)
                    split_low(xl1, xc1, xh1).then_inc(s["x1_lo"], 1)
                if tile_known(m):
                    pool.wait_ge(s["x_loaded"], 16 * m + 16)
                    if isinstance(i, int) and i == 1:
                        pool.wait_ge(s["prep"], PREP_BROW)
                    wait(pool, s["x2_ready"], 4 * m)
                    add_row(xb, x_tile(m), brow[:, :], s["xb_ready"])
                if tile_known(g):
                    pool.wait_ge(s["x2_split"], 2 * g + 2)
                    wait(pool, s["hid_psum"], 3 * g)
                    split_low(xl2, xc2, xh2).then_inc(s["x2_lo"], 1)
                if tile_known(m):
                    pool.wait_ge(s["mvm_ready"], 4 * m + 4)
                    inverse_std(rsm, mvm, eps0, s["lnm_step"], 2 * m)
                    pool.wait_ge(s["mv2_ready"], 4 * m + 4)
                    minus_mean(ng2, mv2, s["ln2_step"])
                    inverse_std(rs2, mv2, eps0, s["ln2_step"], 3 * m + 1)
                    wait(pool, s["x3_ready"], m)
                    pool.wait_ge(s["ln2_step"], 3 * m + 3)
                    wait(pool, s["tr2_done"], m)
                    add_row(x2b, x2[:, :], rows[:, D:2 * D], s["x2b_ready"])
                    normalize(xn2, x2, ng2, rs2, s["xn2_ready"])

            run0(pool, body0)

            def body1(i):
                n, f, m = i + 2, i + 1, i - 1
                if tile_known(m):
                    pool.wait_ge(s["mv4_ready"], 4 * m + 4)
                    wait(pool, s["xn4_ready"], 4 * m)
                    inverse_std(rs4, mv4, eps1, s["ln4_step"], 2 * m)
                if tile_known(f):
                    pool.wait_ge(s["x3_split"], 2 * f + 2)
                    wait(pool, s["ugv_psum"], 3 * f)
                    split_low(xl3, xc3, xh3).then_inc(s["x3_lo"], 1)
                if tile_known(m):
                    pool.wait_ge(s["x4_split"], 2 * m + 2)
                    wait(pool, s["hid1_psum"], 3 * m)
                    split_low(xl4, xc4, xh4).then_inc(s["x4_lo"], 1)
                if tile_known(n):
                    pool.wait_ge(s["mv3_ready"], 4 * n + 4)
                    wait(pool, s["xn3_ready"], 4 * n)
                    inverse_std(rs3, mv3, eps1, s["ln3_step"], 2 * n)
                if tile_known(m):
                    wait(pool, s["y_ready"], m)
                    add_row(x4b, x4[:, :], rows[:, 2 * D:3 * D], s["x4b_ready"])

            run1(pool, body1)

        @block.scalar
        def _(act):
            def split_high(xc, xh, src, done):
                act.activation(xc, src, ACT.Copy).then_inc(done, 1)
                act.activation(xh, src, ACT.Copy).then_inc(done, 1)

            def body0(i):
                n, f, m, g = i + 2, i + 1, i - 1, i - 2
                if tile_known(m):
                    for k in range(2):
                        act.wait_ge(s["ltr_done"], 2 * m + k + 1)
                        if k == 0:
                            wait(act, s["mix_done"], 2 * m)
                        act.activation(local[:, k * 384:(k + 1) * 384], bank[4 + k][:, 0:384],
                                       ACT.Copy).then_inc(s["local_ready"], 1)
                if tile_known(f):
                    act.wait_ge(s["trx_done"], f + 1)
                    wait(act, s["x1_lo"], f)
                    wait(act, s["p_psum"], 2 * f)
                    split_high(xc1[0:D, :].rearrange("c (i p a) -> c i a p", i=2, a=2),
                               xh1[0:D, :].rearrange("c (i p a) -> c i a p", i=2, a=2),
                               bank[0][0:D, :].rearrange("c (i a p) -> c i a p", i=2, a=2), s["x1_split"])
                if tile_known(n):
                    act.wait_ge(s["ln1_step"], 4 * n + 4)
                    act.wait_ge(s["x_loaded"], 16 * n + 16)
                    wait(act, s["trx_done"], n)
                    xt = x_tile(n)
                    for k in range(CHUNKS):
                        act.activation(xn1[:, k * D:(k + 1) * D], xt[:, k * D:(k + 1) * D], ACT.Identity,
                                       bias=ng1[:, k:k + 1], scale=rs1[:, k:k + 1]).then_inc(s["xn1_ready"], 1)
                if tile_known(m):
                    wait(act, s["mtr_done"], m)
                    wait(act, s["mvm_ready"], 4 * m)
                    for a in range(2):
                        act.wait_ge(s["mix_done"], 2 * m + a + 1)
                        act.activation(mixed[:, a * 384:(a + 1) * 384], bank[4 + a][:, 0:384],
                                       ACT.Copy).then_inc(s["mixed_ready"], 1)
                if tile_known(g):
                    act.wait_ge(s["tr2_done"], g + 1)
                    wait(act, s["x2_lo"], g)
                    wait(act, s["hid_psum"], 3 * g)
                    split_high(xc2[0:D, :], xh2[0:D, :], bank[1][0:D, :], s["x2_split"])
                if tile_known(m):
                    act.wait_ge(s["mtr_done"], m + 1)
                    wait(act, s["wout_done"], m)
                    act.activation(mcA[:, :], bank[4][:, :], ACT.Copy).then_inc(s["mc_ready"], 1)
                    act.activation(mcB[:, :], bank[5][:, 0:TOKENS], ACT.Copy).then_inc(s["mc_ready"], 1)
                if tile_known(g):
                    wait(act, s["w2_done"], g)
                    for j in range(HJ):
                        act.wait_ge(s["hid_psum"], 3 * g + j + 1)
                        act.activation(hid[:, j * TILE:(j + 1) * TILE], bank[6 + j % 2][:, :], ACT.Gelu,
                                       bias=B[f"b1_{j}"]).then_inc(s["gelu_done"], 1)
                if tile_known(f):
                    act.wait_ge(s["p_psum"], 2 * f + 2)
                    if isinstance(i, int) and i == -1:
                        act.wait_ge(s["pads_zero"], 4)
                        act.wait_ge(s["prep"], PREP_BIAS0)
                    wait(act, s["conv_step"], 18 * f)
                    inA = pA[:, LEAD:LEAD + 2 * IMG].rearrange("c (i r w) -> c i r w", i=2, w=ROW)
                    act.activation(inA[:, :, 0:SIDE, 0:SIDE],
                                   bank[2][:, :].rearrange("c (i r w) -> c i r w", i=2, w=SIDE),
                                   ACT.Identity, bias=B["inA"]).then_inc(s["p_ready"], 1)
                    inB = pB[:, LEAD:LEAD + IMG].rearrange("c (r w) -> c r w", w=ROW)
                    act.activation(inB[:, 0:SIDE, 0:SIDE],
                                   bank[3][:, 0:TOKENS].rearrange("c (r w) -> c r w", w=SIDE),
                                   ACT.Identity, bias=B["inB"]).then_inc(s["p_ready"], 1)

            act.preload_act_table(ACT.Gelu)
            run0(act, body0)

            def body1(i):
                f, c, m = i + 1, i, i - 1

                def seed(k):
                    wait(act, s["q_ready"], 8 * c + k if k >= 2 else 8 * c)
                    act.activation(bank[k % 2][0:D, :], vh[0:D, :], ACT.Copy).then_inc(s["seeded"], 1)

                def gelu(j):
                    act.wait_ge(s["hid1_psum"], 3 * m + j + 1)
                    act.activation(hid1[:, j * TILE:(j + 1) * TILE], bank[6 + j % 2][:, :],
                                   ACT.Gelu_apprx_tanh, bias=B[f"m1_{j}"]).then_inc(s["gelu1_done"], 1)

                if tile_known(c):
                    wait(act, s["h8_ready"], c)
                    if isinstance(i, int) and i == 0:
                        act.wait_ge(s["bits_set"], 2)
                    act.wait_ge(s["ugv_psum"], 3 * c + 1)
                    act.activation(th[0:D, :], bank[3][0:D, :], ACT.Tanh, bias=B["g_half"][0:D],
                                   scale=0.5).then_inc(s["ugv_ready"], 1)
                    act.wait_ge(s["ugv_psum"], 3 * c + 2)
                    act.activation(nu[0:D, :], bank[4][0:D, :], ACT.Identity, bias=B["u_neg_half"][0:D],
                                   scale=-0.5).then_inc(s["ugv_ready"], 1)
                    act.wait_ge(s["ugv_psum"], 3 * c + 3)
                    act.activation(vh[0:D, :], bank[5][0:D, :], ACT.Identity,
                                   bias=B["v_half"][0:D]).then_inc(s["ugv_ready"], 1)
                    act.wait_ge(s["ugv_ready"], 3 * c + 3)
                    seed(0)
                    seed(1)
                if tile_known(f):
                    act.wait_ge(s["tr3_done"], f + 1)
                    wait(act, s["x3_lo"], f)
                    wait(act, s["ugv_psum"], 3 * f)
                    split_high(xc3[0:D, :], xh3[0:D, :], bank[2][0:D, :], s["x3_split"])
                if tile_known(c):
                    seed(2)
                if tile_known(m):
                    act.wait_ge(s["tr4_done"], m + 1)
                    wait(act, s["x4_lo"], m)
                    wait(act, s["hid1_psum"], 3 * m)
                    split_high(xc4[0:D, :], xh4[0:D, :], bank[2][0:D, :], s["x4_split"])
                if tile_known(c):
                    seed(3)
                    seed(4)
                    seed(5)
                if tile_known(m):
                    wait(act, s["m2_done"], m)
                    gelu(0)
                if tile_known(c):
                    seed(6)
                if tile_known(m):
                    gelu(1)
                    gelu(2)

            act.preload_act_table(ACT.Gelu_apprx_tanh)
            run1(act, body1)

        @block.vector
        def _(dve):
            def stats(st, mv, chunk, step, ready, t, between=lambda: None):
                for k in range(CHUNKS):
                    dve.bn_stats(st[:, 6 * k:6 * k + 6], chunk(k)).then_inc(step, 1)
                dve.wait_ge(step, 4 * t + 4)
                between()
                for k in range(CHUNKS):
                    dve.bn_aggr(mv[:, 2 * k:2 * k + 2], st[:, 6 * k:6 * k + 6]).then_inc(ready, 1)

            count = [0]

            def prep(instruction):
                count[0] += 1
                instruction.then_inc(s["prep"], 1)
                return count[0]

            def split_weight(v, hi, lo, width, done):
                dve.wait_ge(s["prep"], done)
                high = prep(dve.tensor_copy(hi[0:D, 0:width], v[0:D, 0:width]))
                dve.wait_ge(s["prep"], high)
                return prep(dve.tensor_tensor(lo[0:D, 0:width], v[0:D, 0:width],
                                              hi[0:D, 0:width].bitcast(F32), ALU.subtract))

            def w0s(name, n=P):
                return w0[0:n, W0[name][0]:W0[name][1]]

            def w1s(name, n=P):
                return w1[0:n, W1[name][0]:W1[name][1]]

            def scaled(res, v, factor, scale2=None):
                return prep(dve.tensor_scalar(res, v, factor, scale2, ALU.mult, ALU.bypass if scale2 is None else ALU.mult))

            def setup0():
                dve.wait_ge(s["w0_loaded"], 80)
                dve.wait_ge(s["ones_set"], 1)
                scaled(onbA[:, :], ones[:, :], col("on_bA"))
                scaled(onbB[:, :], ones[:, :], col("on_bB"))
                scaled(woA_f[:, :], w0s("w_outA"), col("on_gA"))
                done = scaled(woB_f[:, :], w0s("w_outB"), col("on_gB"))
                assert done == PREP_WOUT
                done = scaled(wi_f[0:D, :], w0s("w_in", D), col("n1_g", D))
                done = split_weight(wi_f, wi_h, wi_l, 384, done)
                assert done == PREP_WIN
                dve.wait_ge(s["prep_psum"], 1)
                for k, name in enumerate(("inA", "inB", "b1_0", "b1_1", "b1_2")):
                    done = prep(dve.tensor_tensor(B[name], bank[0][:, k:k + 1],
                                                  col({"inA": "b_inA", "inB": "b_inB"}.get(name, name)), ALU.add))
                assert done == PREP_BIAS0
                dve.wait_ge(s["prep_psum"], 2)
                done = prep(dve.tensor_tensor(brow[:, :], bank[1][:, 0:D], rows[:, 0:D], ALU.add))
                assert done == PREP_BROW
                dve.wait_ge(s["prep_psum"], 3)
                dve.wait_ge(s["pads_zero"], 4)
                for res, v, lo, hi in ((woA, woA_f, 0, P), (woB0, woB_f, 0, HB), (woB1, woB_f, HB, P)):
                    done = prep(dve.scalar_tensor_tensor(out=res[lo:hi, :], in0=bank[2][lo:hi, 0:D],
                                                         scalar=-1.0 / INNER, in1=v[lo:hi, :],
                                                         op0=ALU.mult, op1=ALU.add))
                assert done == PREP_WOC
                done = scaled(w1_f[0:D, :], w0s("w1", D), col("n2_g", D))
                done = split_weight(w1_f, w1_h, w1_l, 384, done)
                assert done == PREP_W1

            def setup1():
                dve.wait_ge(s["w1_loaded"], 16)
                prep(dve.tensor_tensor(a_i[0:D, :], w1s("A", D), ident[0:D, 0:D], ALU.subtract))
                done = scaled(a_half[0:D, :], w1s("A", D), 0.5)
                dve.wait_ge(s["prep_psum"], 4)
                done = prep(dve.tensor_copy(wuT[0:D, :], bank[4][0:D, 0:D]))
                assert done == PREP_WUT
                dve.wait_ge(s["prep_psum"], 5)
                bu = prep(dve.tensor_tensor(B["u"][0:D], bank[6][0:D, 0:1], col("bu", D), ALU.add))
                assert bu == PREP_BU
                bg = prep(dve.tensor_tensor(B["g_half"][0:D], bank[6][0:D, 1:2], col("bg", D), ALU.add))
                for j in range(HJ):
                    prep(dve.tensor_tensor(B[f"m1_{j}"], bank[6][:, 2 + j:3 + j], col(f"m1_{j}"), ALU.add))
                dve.wait_ge(s["prep"], bg)
                scaled(B["u_neg_half"][0:D], B["u"][0:D], -0.5)
                scaled(B["g_half"][0:D], B["g_half"][0:D], 0.5)
                scaled(w3_f[0:D, 0:2 * D], w1[0:D, 0:2 * D], col("s3", D))
                dve.wait_ge(s["prep_psum"], 6)
                done = scaled(w3_f[0:D, 2 * D:3 * D], bank[5][0:D, 0:D], col("s3", D), 0.5)
                split_weight(w3_f, w3_h, w3_l, 3 * D, done)
                dve.wait_ge(s["prep_psum"], 7)
                scaled(B["v_half"][0:D], bank[7][0:D, 0:1], 0.5)
                done = scaled(m1_f[0:D, :], w1s("m1", D), col("s4", D))
                done = split_weight(m1_f, m1_h, m1_l, 384, done)
                assert done == PREP_ALL

            def body0(i):
                n, c, m, g = i + 2, i, i - 1, i - 2

                def tap(k):
                    if not tile_known(c):
                        return
                    dy, dx = TAPS[k]
                    at = LEAD + dy * ROW + dx
                    srcA = pA[:, at:at + (2 * SIDE + 1) * ROW].rearrange("c (r w) -> c r w", w=ROW)[:, :, 0:SIDE]
                    srcB = pB[:, at:at + SIDE * ROW].rearrange("c (r w) -> c r w", w=ROW)[:, :, 0:SIDE]
                    for grp, (acc, src, kc) in enumerate(((cA, srcA, col(f"kA{k}")), (cB, srcB, col(f"kB{k}")))):
                        acc = acc[:, :].rearrange("c (r w) -> c r w", w=SIDE)
                        if k == 0:
                            dve.wait_ge(s["p_ready"], 2 * c + 1 + grp)
                            dve.tensor_scalar(acc, src, kc, None, ALU.mult).then_inc(s["conv_step"], 1)
                        else:
                            dve.wait_ge(s["conv_step"], 18 * c + 2 * k - 1 + grp)
                            dve.scalar_tensor_tensor(out=acc, in0=src, scalar=kc, in1=acc,
                                                     op0=ALU.mult, op1=ALU.add).then_inc(s["conv_step"], 1)

                if tile_known(c):
                    wait(dve, s["ltr_done"], 2 * c)
                if tile_known(n):
                    dve.wait_ge(s["x_loaded"], 16 * n + 16)
                    wait(dve, s["ln1_step"], 4 * n)
                    xt = x_tile(n)
                    stats(st1, mv1, lambda k: xt[:, k * D:(k + 1) * D], s["bn1_step"], s["mv1_ready"], n,
                          between=lambda: tap(0))
                else:
                    tap(0)
                for k in range(1, 4):
                    tap(k)
                if tile_known(m):
                    dve.wait_ge(s["mixed_ready"], 2 * m + 2)
                    wait(dve, s["lnm_step"], 2 * m)
                    stats(stm, mvm, lambda k: mixed[:, (k % 2) * 384 + (k // 2) * INNER:(k % 2) * 384 + (k // 2 + 1) * INNER],
                          s["bnm_step"], s["mvm_ready"], m, between=lambda: tap(4))
                else:
                    tap(4)
                for k in range(5, 7):
                    tap(k)
                tap(7)
                if tile_known(m):
                    dve.wait_ge(s["xb_ready"], m + 1)
                    dve.wait_ge(s["lnm_step"], 2 * m + 2)
                    wait(dve, s["xn2_ready"], 4 * m)
                    wait(dve, s["x2b_ready"], m)
                    dve.wait_ge(s["wout_done"], m + 1)
                    for k in range(CHUNKS):
                        dve.scalar_tensor_tensor(out=x2[:, k * D:(k + 1) * D], in0=bank[1][:, k * D:(k + 1) * D],
                                                 scalar=rsm[:, k:k + 1], in1=xb[:, k * D:(k + 1) * D],
                                                 op0=ALU.mult, op1=ALU.add).then_inc(s["x2_ready"], 1)
                    wait(dve, s["ln2_step"], 3 * m)
                    dve.wait_ge(s["x2_ready"], 4 * m + 4)
                    stats(st2, mv2, lambda k: x2[:, k * D:(k + 1) * D], s["bn2_step"], s["mv2_ready"], m,
                          between=lambda: tap(8))
                else:
                    tap(8)
                if tile_known(g):
                    dve.wait_ge(s["x2b_ready"], g + 1)
                    dve.wait_ge(s["w2_done"], g + 1)
                    dve.tensor_tensor(x_tile(g), bank[0][:, 0:384], x2b[:, :], ALU.add).then_inc(s["x3_ready"], 1)

            body0(-2)
            setup0()
            body0(-1)
            setup1()
            run(dve, body0, 0, 2, TILES - 2, TILES + 2)

            def body1(i):
                n, c, m, g = i + 2, i, i - 1, i - 2
                def step(k):
                    if tile_known(c):
                        dve.wait_ge(s["step_done"], 7 * c + k + 1)
                        dve.scalar_tensor_tensor(out=q[0:D, :], in0=th[0:D, :], scalar=1.0, in1=bank[k % 2][0:D, :],
                                                 op0=ALU.add, op1=ALU.mult).then_inc(s["q_ready"], 1)

                def normalize(xn, v, mv, rs, ready):
                    for k in range(CHUNKS):
                        dve.tensor_scalar(xn[:, k * D:(k + 1) * D], v[:, k * D:(k + 1) * D],
                                          mv[:, 2 * k:2 * k + 1], rs[:, k:k + 1],
                                          ALU.subtract, ALU.mult).then_inc(ready, 1)

                if tile_known(c):
                    dve.wait_ge(s["ugv_ready"], 3 * c + 2)
                    dve.scalar_tensor_tensor(out=q[0:D, :], in0=th[0:D, :], scalar=1.0, in1=nu[0:D, :],
                                             op0=ALU.add, op1=ALU.mult).then_inc(s["q_ready"], 1)
                if tile_known(m):
                    dve.wait_ge(s["trh_done"], m + 1)
                    wait(dve, s["xn4_ready"], 4 * m)
                    wait(dve, s["x4b_ready"], m)
                    dve.tensor_tensor(x4[:, :], bank[2][:, 0:384], x_tile(m), ALU.add).then_inc(s["x4_ready"], 1)
                    wait(dve, s["ln4_step"], 2 * m)
                    dve.wait_ge(s["x4_ready"], m + 1)
                    stats(st4, mv4, lambda k: x4[:, k * D:(k + 1) * D], s["bn4_step"], s["mv4_ready"], m,
                          between=lambda: step(0))
                else:
                    step(0)
                if tile_known(n):
                    dve.wait_ge(s["x3_ready"], n + 1)
                    wait(dve, s["ln3_step"], 2 * n)
                    wait(dve, s["xn3_ready"], 4 * n)
                    xt = x_tile(n)
                    stats(st3, mv3, lambda k: xt[:, k * D:(k + 1) * D], s["bn3_step"], s["mv3_ready"], n,
                          between=lambda: step(1))
                else:
                    step(1)
                if tile_known(m):
                    dve.wait_ge(s["ln4_step"], 2 * m + 2)
                    wait(dve, s["tr4_done"], m)
                    normalize(xn4, x4, mv4, rs4, s["xn4_ready"])
                if tile_known(g):
                    dve.wait_ge(s["x4b_ready"], g + 1)
                    wait(dve, s["y_stored"], 16 * g)
                    dve.wait_ge(s["m2_done"], g + 1)
                    dve.tensor_tensor(y[:, :], bank[7][:, 0:384], x4b[:, :], ALU.add).then_inc(s["y_ready"], 1)
                for k in range(2, 6):
                    step(k)
                if tile_known(n):
                    dve.wait_ge(s["ln3_step"], 2 * n + 2)
                    wait(dve, s["tr3_done"], n)
                    normalize(xn3, xt, mv3, rs3, s["xn3_ready"])
                step(6)
                if tile_known(c):
                    wait(dve, s["trh_done"], c)
                    dve.wait_ge(s["q_ready"], 8 * c + 8)
                    dve.scalar_tensor_tensor(out=h8[0:D, :], in0=nu[0:D, :], scalar=-2.0, in1=q[0:D, :],
                                             op0=ALU.mult, op1=ALU.add).then_inc(s["h8_ready"], 1)

            run1(dve, body1)

        @block.tensor
        def _(pe):
            def wc0(name, lo=0, hi=None, n=P):
                a, b = W0[name]
                return w0[0:n, a + lo:b if hi is None else a + hi]

            def wc1(name, lo=0, hi=None, n=P):
                a, b = W1[name]
                return w1[0:n, a + lo:b if hi is None else a + hi]

            def setup0():
                pe.wait_ge(s["w0_loaded"], 80)
                pe.matmul(bank[0][:, 0:1], wc0("w_in", 0, 128, D), col("n1_b", D), start=True, stop=True)
                pe.matmul(bank[0][:, 1:2], wc0("w_in", 128, 256, D), col("n1_b", D), start=True, stop=False)
                pe.matmul(bank[0][:, 1:2], wc0("w_in", 256, 384, D), col("n1_b", D), start=False, stop=True)
                for j in range(HJ):
                    last = pe.matmul(bank[0][:, 2 + j:3 + j], wc0("w1", j * P, (j + 1) * P, D), col("n2_b", D),
                                     start=True, stop=True)
                last.then_inc(s["prep_psum"], 1)
                pe.wait_ge(s["prep"], PREP_WOUT)
                pe.matmul(bank[1][:, 0:D], onbA[:, :], wc0("w_outA"), start=True, stop=False)
                pe.matmul(bank[1][:, 0:D], onbB[0:HB, :], wc0("w_outB", n=HB), start=False, stop=True)\
                  .then_inc(s["prep_psum"], 1)
                pe.matmul(bank[2][:, 0:D], ones[:, :], woA_f[:, :], start=True, stop=False)
                pe.matmul(bank[2][:, 0:D], ones[0:HB, :], woB_f[0:HB, :], start=False, stop=True)\
                  .then_inc(s["prep_psum"], 1)

            def setup1():
                pe.wait_ge(s["w1_loaded"], 16)
                pe.transpose(bank[4][0:D, 0:D], wc1("Wu", n=D), ident[0:D, 0:D]).then_inc(s["prep_psum"], 1)
                pe.matmul(bank[6][0:D, 0:1], wc1("Wu", n=D), col("c3", D), start=True, stop=True)
                pe.matmul(bank[6][0:D, 1:2], wc1("Wg", n=D), col("c3", D), start=True, stop=True)
                for j in range(HJ):
                    last = pe.matmul(bank[6][:, 2 + j:3 + j], wc1("m1", j * P, (j + 1) * P, D), col("c4", D),
                                     start=True, stop=True)
                last.then_inc(s["prep_psum"], 1)
                pe.wait_ge(s["prep"], PREP_WUT)
                pe.matmul(bank[5][0:D, 0:D], wuT[0:D, :], a_i[0:D, :], start=True, stop=True).then_inc(s["prep_psum"], 1)
                pe.wait_ge(s["prep"], PREP_BU)
                pe.matmul(bank[7][0:D, 0:1], a_i[0:D, :], B["u"][0:D], start=True, stop=True).then_inc(s["prep_psum"], 1)

            def transposes(dst, src, done):
                for k in range(CHUNKS):
                    last = pe.transpose(dst[0:D, k * P:(k + 1) * P], src[:, k * D:(k + 1) * D], ident[:, :])
                last.then_inc(done, 1)

            def three_passes(dst, wh, wl, xh, xl, first=True, last=True):
                pe.matmul(dst, wh, xh, start=first, stop=False)
                pe.matmul(dst, wh, xl, start=False, stop=False)
                return pe.matmul(dst, wl, xh, start=False, stop=last)

            def body0(i):
                f, m, g = i + 1, i - 1, i - 2
                if isinstance(i, int) and i == 1:
                    pe.wait_ge(s["prep"], PREP_ALL)
                def w1(j):
                    if tile_known(g):
                        if j == 0:
                            pe.wait_ge(s["x2_lo"], g + 1)
                            pe.wait_ge(s["x2_split"], 2 * g + 2)
                        wait(pe, s["gelu_done"], 3 * g + max(j - 1, 0))
                        w = slice(P * j, P * (j + 1))
                        three_passes(bank[6 + j % 2][:, :], w1_h[0:D, w], w1_l[0:D, w], xh2[0:D, :], xl2[0:D, :])\
                            .then_inc(s["hid_psum"], 1)

                if tile_known(m):
                    pe.wait_ge(s["conv_step"], 18 * m + 18)
                    wait(pe, s["mc_ready"], 2 * m)
                    for k in range(2):
                        for part, src in enumerate((cA[:, k * P:(k + 1) * P], cB[:, k * P:(k + 1) * P],
                                                    cA[:, 272 + k * P:272 + (k + 1) * P])):
                            last = pe.transpose(bank[4 + k][:, part * P:(part + 1) * P], src, ident[:, :])
                        last.then_inc(s["ltr_done"], 1)
                if tile_known(f):
                    pe.wait_ge(s["xn1_ready"], 4 * f + 4)
                    wait(pe, s["x3_ready"], f - 3)
                    if isinstance(i, int) and i == -1:
                        pe.wait_ge(s["prep"], PREP_BIAS0)
                    transposes(bank[0], xn1, s["trx_done"])
                if tile_known(m):
                    pe.wait_ge(s["local_ready"], 2 * m + 2)
                    for a in range(2):
                        for k in range(2):
                            last = pe.matmul(bank[4 + a][:, 0:384],
                                             mix[:, k * TOKENS + a * P:k * TOKENS + (a + 1) * P],
                                             local[:, k * 384:(k + 1) * 384], start=(k == 0), stop=(k == 1))
                        last.then_inc(s["mix_done"], 1)
                if tile_known(g):
                    pe.wait_ge(s["xn2_ready"], 4 * g + 4)
                    pe.wait_ge(s["x2_ready"], 4 * g + 4)
                    transposes(bank[1], xn2, s["tr2_done"])
                if tile_known(f):
                    pe.wait_ge(s["x1_lo"], f + 1)
                    pe.wait_ge(s["x1_split"], 2 * f + 2)
                    if isinstance(i, int) and i == -1:
                        pe.wait_ge(s["prep"], PREP_WOC)
                    wait(pe, s["p_ready"], 2 * f)
                    three_passes(bank[2][:, :], wi_h[0:D, 0:P], wi_l[0:D, 0:P], xh1[0:D, :], xl1[0:D, :])\
                        .then_inc(s["p_psum"], 1)
                    for im in range(2):
                        w = slice(P * (im + 1), P * (im + 2))
                        x_ = slice(TOKENS * im, TOKENS * (im + 1))
                        last = three_passes(bank[3][:, 0:TOKENS], wi_h[0:D, w], wi_l[0:D, w], xh1[0:D, x_],
                                            xl1[0:D, x_], first=(im == 0), last=(im == 1))
                    last.then_inc(s["p_psum"], 1)
                if tile_known(m):
                    pe.wait_ge(s["mixed_ready"], 2 * m + 2)
                    for im in range(2):
                        for a in range(2):
                            src = mixed[:, a * 384 + 2 * P * im:a * 384 + 2 * P * im + P]
                            k = 2 * im + a
                            pe.transpose(bank[4][:, k * P:(k + 1) * P], src, ident[:, :])
                    for a in range(2):
                        last = pe.transpose(bank[5][:, a * P:(a + 1) * P], mixed[:, a * 384 + P:a * 384 + 2 * P],
                                            ident[:, :])
                    last.then_inc(s["mtr_done"], 1)
                w1(0)
                if tile_known(m):
                    pe.wait_ge(s["mc_ready"], 2 * m + 2)
                    wait(pe, s["x2_split"], 2 * m)
                    for k in range(CHUNKS):
                        im, a = k // 2, k % 2
                        pe.matmul(bank[1][:, k * D:(k + 1) * D], mcA[:, k * P:(k + 1) * P], woA[:, :],
                                  start=True, stop=False)
                        last = pe.matmul(bank[1][:, k * D:(k + 1) * D], mcB[:, a * P:(a + 1) * P],
                                         (woB0, woB1)[im][:, :], start=False, stop=True)
                    last.then_inc(s["wout_done"], 1)
                w1(1)
                w1(2)
                if tile_known(g):
                    if tile_known(f):
                        pe.wait_ge(s["x1_split"], 2 * f + 2)
                    for j in range(HJ):
                        pe.wait_ge(s["gelu_done"], 3 * g + j + 1)
                        for k in range(CHUNKS):
                            last = pe.matmul(bank[0][:, k * D:(k + 1) * D],
                                             hid[:, j * TILE + k * P:j * TILE + (k + 1) * P],
                                             wc0("w2", j * D, (j + 1) * D), start=(j == 0 and k == 0),
                                             stop=(j == HJ - 1), skip_group_check=True)
                    last.then_inc(s["w2_done"], 1)

            setup0()
            body0(-2)
            body0(-1)
            setup1()
            run(pe, body0, 0, 2, TILES - 2, TILES + 2)

            pe.wait_ge(s["x3_ready"], TILES)
            for b in range(2):
                pe.matmul(bank[b][0:D, :], a_half[0:D, :], xc1[0:D, :], start=True, stop=True)\
                  .then_inc(s["bits_set"], 1)

            def body1(i):
                f, c, m, g = i + 1, i, i - 1, i - 2
                def step(k):
                    if tile_known(c):
                        pe.wait_ge(s["seeded"], 7 * c + k + 1)
                        pe.wait_ge(s["q_ready"], 8 * c + k + 1)
                        pe.matmul(bank[k % 2][0:D, :], a_half[0:D, :], q[0:D, :], start=False, stop=True,
                                  skip_group_check=True).then_inc(s["step_done"], 1)

                if tile_known(m):
                    pe.wait_ge(s["h8_ready"], m + 1)
                    wait(pe, s["x4_split"], 2 * m)
                    for k in range(CHUNKS):
                        last = pe.transpose(bank[2][:, k * D:(k + 1) * D], h8[0:D, k * P:(k + 1) * P],
                                            ident[0:D, 0:D])
                    last.then_inc(s["trh_done"], 1)
                step(0)
                if tile_known(g):
                    for j in range(HJ):
                        pe.wait_ge(s["gelu1_done"], 3 * g + max(j + 1, 2))
                        for k in range(CHUNKS):
                            last = pe.matmul(bank[7][:, k * D:(k + 1) * D],
                                             hid1[:, j * TILE + k * P:j * TILE + (k + 1) * P],
                                             wc1("m2", j * D, (j + 1) * D), start=(j == 0 and k == 0),
                                             stop=(j == HJ - 1), skip_group_check=True)
                    last.then_inc(s["m2_done"], 1)

                def ugv(k):
                    if tile_known(f):
                        if k == 0:
                            pe.wait_ge(s["x3_lo"], f + 1)
                            pe.wait_ge(s["x3_split"], 2 * f + 2)
                            wait(pe, s["ugv_ready"], 3 * f)
                        w = slice((1, 0, 2)[k] * D, ((1, 0, 2)[k] + 1) * D)
                        three_passes(bank[3 + k][0:D, :], w3_h[0:D, w], w3_l[0:D, w], xh3[0:D, :], xl3[0:D, :])\
                            .then_inc(s["ugv_psum"], 1)

                def m1(j):
                    if tile_known(m):
                        if j == 0:
                            pe.wait_ge(s["x4_lo"], m + 1)
                            pe.wait_ge(s["x4_split"], 2 * m + 2)
                        wait(pe, s["gelu1_done"], 3 * m + max(j - 1, 0))
                        if j == 1:
                            wait(pe, s["y_ready"], m)
                        w = slice(P * j, P * (j + 1))
                        three_passes(bank[6 + j % 2][:, :], m1_h[0:D, w], m1_l[0:D, w], xh4[0:D, :], xl4[0:D, :])\
                            .then_inc(s["hid1_psum"], 1)

                if tile_known(f):
                    pe.wait_ge(s["xn3_ready"], 4 * f + 4)
                    wait(pe, s["x4_ready"], f - 1)
                    transposes(bank[2], xn3, s["tr3_done"])
                step(1)
                if tile_known(m):
                    pe.wait_ge(s["xn4_ready"], 4 * m + 4)
                    pe.wait_ge(s["x4_ready"], m + 1)
                    if tile_known(f):
                        pe.wait_ge(s["x3_split"], 2 * f + 2)
                    transposes(bank[2], xn4, s["tr4_done"])
                step(2)
                ugv(0)
                step(3)
                ugv(1)
                step(4)
                ugv(2)
                m1(0)
                step(5)
                m1(1)
                step(6)
                m1(2)

            run1(pe, body1)


PREP_WOUT = 4
PREP_WIN = 7
PREP_BIAS0 = 12
PREP_BROW = 13
PREP_WOC = 16
PREP_W1 = 19
PREP_WUT = 22
PREP_BU = 23
PREP_ALL = 37


VECTORS = {
    "n1_g": "L0_conv_n1_g", "n1_b": "L0_conv_n1_b", "n2_g": "L0_conv_n2_g", "n2_b": "L0_conv_n2_b",
    "s3": "L1_conv_norm1_scale", "c3": "L1_conv_norm1_bias", "bu": "L1_conv_bu", "bg": "L1_conv_bg",
    "s4": "L1_conv_norm2_scale", "c4": "L1_conv_norm2_bias"}


def kernel(**inputs):
    import numpy as np
    import concourse.bacc as bacc
    from concourse.bass_utils import run_bass_kernel_spmd

    a = {k: np.asarray(v) for k, v in inputs.items()}
    cols = np.zeros((P, len(COLS)), np.float32)

    def put(name, v):
        cols[:len(v), COLS.index(name)] = v

    def put_inner(name, v):
        k = {"k": lambda g: name.replace("?", g)}["k"]
        put(k("A"), v[:P])
        put(k("B"), np.concatenate([v[P:], v[P:]]))

    for name, source in VECTORS.items():
        put(name, a[source])
    put_inner("b_in?", a["L0_conv_b_in"])
    put_inner("on_g?", a["L0_conv_on_g"])
    put_inner("on_b?", a["L0_conv_on_b"])
    taps = a["L0_conv_k_conv"].reshape(9, INNER)
    for t in range(9):
        put_inner(f"k?{t}", taps[t])
    for j in range(HJ):
        put(f"b1_{j}", a["L0_conv_b1"][j * P:(j + 1) * P])
        put(f"m1_{j}", a["L1_conv_mlp_b1"][j * P:(j + 1) * P])
    rows = np.concatenate([a["L0_conv_b_out"], a["L0_conv_b2"], a["L1_conv_mlp_b2"]])[None, :]

    w0 = np.zeros((P, 1248), np.float32)
    w0[:D, 0:P] = a["L0_conv_w_in"][:, :P]
    w0[:D, P:P + HB] = a["L0_conv_w_in"][:, P:]
    w0[:D, 2 * P + HB:3 * P] = a["L0_conv_w_in"][:, P:]
    w0[:, 384:480] = a["L0_conv_w_out"][:P]
    w0[:, 480:576] = np.concatenate([a["L0_conv_w_out"][P:]] * 2)
    w0[:D, 576:960] = a["L0_conv_w1"]
    w0[:, 960:1248] = a["L0_conv_w2"].reshape(HJ, P, D).transpose(1, 0, 2).reshape(P, HJ * D)
    w1 = np.zeros((P, 960), np.float32)
    w1[:D, 0:96] = a["L1_conv_Wu"]
    w1[:D, 96:192] = a["L1_conv_Wg"]
    w1[:D, 192:288] = a["L1_conv_A"]
    w1[:D, 288:672] = a["L1_conv_mlp_w1"]
    w1[:, 672:960] = a["L1_conv_mlp_w2"].reshape(HJ, P, D).transpose(1, 0, 2).reshape(P, HJ * D)

    at = np.arange(SIDE)
    both_ways = GAIN * DECAY ** np.abs(at[:, None] - at[None, :]) * (1 + (at[:, None] == at[None, :]))
    eye = np.eye(SIDE)
    mix = np.eye(TOKENS) + 0.25 * (np.kron(eye, both_ways) + np.kron(both_ways, eye))
    mix = mix.reshape(TOKENS, P, 2).transpose(0, 2, 1).reshape(TOKENS, TOKENS).astype(np.float32)

    arrays = {"x": np.ascontiguousarray(a["x"].reshape(IMAGES * P, 2 * D)), "cols": cols, "rows": rows, "w0": w0,
              "w1": w1, "mix": mix, "ident": np.eye(P, dtype=np.float32)}
    nc = bacc.Bacc("TRN2", target_bir_lowering=False, num_devices=1)
    args = [nc.dram_tensor(f"in_{n}", v.shape, F32, kind="ExternalInput").ap() for n, v in arrays.items()]
    out = nc.dram_tensor("out", (IMAGES * P, 2 * D), F32, kind="ExternalOutput").ap()
    build(nc, *args, out)
    r = run_bass_kernel_spmd(nc, [{f"in_{n}": v for n, v in arrays.items()}], core_ids=[0])
    return r.results[0]["out"].reshape(IMAGES, SIDE, SIDE, D)
```

```python
from contextlib import ExitStack

import concourse.bass as bass
from concourse import mybir

F32 = mybir.dt.float32
F32R = mybir.dt.float32r
ALU = mybir.AluOpType
ACT = mybir.ActivationFunctionType

IMAGES, SIDE, D = 16, 16, 96
INNER, HIDDEN, STEPS = 2 * D, 4 * D, 8
DECAY, GAIN = 0.6, 0.4
P = 128
TOKENS = SIDE * SIDE
TILES = IMAGES // 2
TILE = 2 * TOKENS
CHUNKS = TILE // P
HB = INNER - P
HJ = HIDDEN // P
ROW = SIDE + 1
IMG = ROW * ROW
LEAD = ROW + 1
TAPS = [(dy, dx) for dy in (-1, 0, 1) for dx in (-1, 0, 1)]
EPS0, EPS1 = 1e-5, 1e-6

COLS = (["n1_g", "n1_b", "b_inA", "b_inB"] + [f"kA{t}" for t in range(9)] + [f"kB{t}" for t in range(9)]
        + ["on_gA", "on_gB", "on_bA", "on_bB", "n2_g", "n2_b", "b1_0", "b1_1", "b1_2",
           "s3", "c3", "bu", "bg", "s4", "c4", "m1_0", "m1_1", "m1_2"])
W0 = {"w_in": (0, 384), "w_outA": (384, 480), "w_outB": (480, 576), "w1": (576, 960), "w2": (960, 1248)}
W1 = {"Wu": (0, 96), "Wg": (96, 192), "A": (192, 288), "m1": (288, 672), "m2": (672, 960)}


def tile_known(t):
    return not isinstance(t, int) or 0 <= t < TILES


def wait(engine, sem, count):
    if not isinstance(count, int) or count > 0:
        engine.wait_ge(sem, count)


def build(nc, x, cols_d, rows_d, w0_d, w1_d, mix_d, ident_d, out):
    x_d = x.rearrange("(t i p) f -> t p i f", i=2, p=P)
    out_d = out.rearrange("(t i p) f -> t p i f", i=2, p=P)

    with ExitStack() as ctx:
        def sb(name, cols, dt=F32, rows=P):
            return ctx.enter_context(nc.sbuf_tensor(name, [rows, cols], dt))

        def sem(name):
            return ctx.enter_context(nc.semaphore(name))

        bank = [ctx.enter_context(nc.psum_tensor(f"bank{b}", [P, 512], F32)) for b in range(8)]

        cols = sb("cols", len(COLS))
        rows = sb("rows", 3 * D)
        w0 = sb("w0", 1248)
        w1 = sb("w1", 960)
        mix = sb("mix", 2 * TOKENS)
        ident = sb("ident", P)
        ones = sb("ones", P)
        onbA, onbB = sb("onbA", P), sb("onbB", P)
        wi_f, w1_f, m1_f, w3_f = sb("wi_f", 384), sb("w1_f", 384), sb("m1_f", 384), sb("w3_f", 288)
        wi_h, w1_h, m1_h, w3_h = (sb(n, c, F32R) for n, c in (("wi_h", 384), ("w1_h", 384), ("m1_h", 384), ("w3_h", 288)))
        wi_l, w1_l, m1_l, w3_l = (sb(n, c, F32R) for n, c in (("wi_l", 384), ("w1_l", 384), ("m1_l", 384), ("w3_l", 288)))
        woA_f, woB_f = sb("woA_f", D), sb("woB_f", D)
        woA, woB0, woB1 = sb("woA", D), sb("woB0", D), sb("woB1", D)
        a_i, a_half, wuT = sb("a_i", D), sb("a_half", D), sb("wuT", D)
        bias = sb("bias", 16)
        brow = sb("brow", D)
        B = {n: bias[:, k:k + 1] for k, n in enumerate(
            ["inA", "inB", "b1_0", "b1_1", "b1_2", "m1_0", "m1_1", "m1_2", "u", "u_neg_half", "g_half", "v_half"])}

        def col(name, n=P):
            k = COLS.index(name)
            return cols[0:n, k:k + 1]

        x_all = sb("x_all", TILES * CHUNKS * D)
        st1, mv1, rs1, ng1 = sb("st1", 24), sb("mv1", 8), sb("rs1", 4), sb("ng1", 4)
        st2, mv2, rs2, ng2 = sb("st2", 24), sb("mv2", 8), sb("rs2", 4), sb("ng2", 4)
        stm, mvm, rsm = sb("stm", 24), sb("mvm", 8), sb("rsm", 4)
        st3, mv3, rs3 = sb("st3", 24), sb("mv3", 8), sb("rs3", 4)
        st4, mv4, rs4, ng4 = sb("st4", 24), sb("mv4", 8), sb("rs4", 4), sb("ng4", 4)
        power, minus, eps0, eps1 = (sb(n, 4) for n in ("power", "minus", "eps0", "eps1"))
        xn1, xn2, xn3, xn4 = (sb(f"xn{k}", CHUNKS * D) for k in (1, 2, 3, 4))
        xc1, xc2, xc3, xc4 = (sb(f"xc{k}", TILE) for k in (1, 2, 3, 4))
        xh1, xh2, xh3, xh4 = (sb(f"xh{k}", TILE, F32R) for k in (1, 2, 3, 4))
        xl1, xl2, xl3, xl4 = (sb(f"xl{k}", TILE, F32R) for k in (1, 2, 3, 4))
        SPAN_A, SPAN_B = LEAD + 2 * IMG + LEAD, LEAD + IMG + LEAD
        pA, pB = sb("pA", SPAN_A), sb("pB", SPAN_B)
        cA, cB = sb("cA", (2 * SIDE + 1) * SIDE), sb("cB", TOKENS)
        local = sb("local", 2 * 2 * INNER)
        mixed = sb("mixed", 2 * 2 * INNER)
        mcA, mcB = sb("mcA", TILE), sb("mcB", TOKENS)
        xb, x2 = sb("xb", CHUNKS * D), sb("x2", CHUNKS * D)
        hid = sb("hid", HJ * TILE)
        th, nu, vh, q, h8 = (sb(n, TILE) for n in ("th", "nu", "vh", "q", "h8"))
        x4, x4b, y = sb("x4", CHUNKS * D), sb("x4b", CHUNKS * D), sb("y", CHUNKS * D)
        hid1 = sb("hid1", HJ * TILE)

        s = {n: sem(n) for n in (
            "w0_loaded", "w1_loaded", "ones_set", "pads_zero", "prep", "prep_psum",
            "x_loaded", "bn1_step", "mv1_ready", "ln1_step", "xn1_ready", "trx_done", "x1_split", "x1_lo",
            "p_psum", "p_ready", "tap0_done", "conv_step", "cT_done", "local_ready", "mix_done", "mixed_ready",
            "bnm_step", "mvm_ready", "lnm_step", "mtr_done", "mc_ready", "wout_done", "xb_ready", "x2_ready",
            "bn2_step", "mv2_ready", "ln2_step", "xn2_ready", "x2b_ready", "tr2_done", "x2_split", "x2_lo",
            "hid_psum", "gelu_done", "w2_done", "x3_ready",
            "bn3_step", "mv3_ready", "ln3_step", "xn3_ready", "tr3_done", "x3_split", "x3_lo", "ugv_psum",
            "ugv_ready", "bits_set", "seeded", "step_done", "q_ready", "h8_ready", "trh_done", "x4_ready",
            "bn4_step", "mv4_ready", "ln4_step", "xn4_ready", "x4b_ready", "tr4_done", "x4_split", "x4_lo",
            "hid1_psum", "gelu1_done", "m2_done", "y_ready", "y_stored")}

        block = ctx.enter_context(nc.Block())

        def x_tile(t):
            return x_all[:, bass.ts(t, CHUNKS * D)]

        def half(h):
            return slice(h * TOKENS, (h + 1) * TOKENS)

        def rec(k, h):
            return bank[2 * h + k % 2][0:D, 0:TOKENS]

        def run(engine, body, first, steady, after, last):
            for i in range(first, steady):
                body(i)
            with engine.Fori(steady, after) as i:
                body(i)
            for i in range(after, last):
                body(i)

        def run0(engine, body):
            run(engine, body, -2, 3, TILES - 2, TILES + 3)

        def run1(engine, body):
            run(engine, body, -2, 2, TILES - 2, TILES + 2)

        def tap_views(k):
            dy, dx = TAPS[k]
            at = LEAD + dy * ROW + dx
            shifted = (pA[:, at:at + (2 * SIDE + 1) * ROW], pB[:, at:at + SIDE * ROW])
            return [(acc[:, :].rearrange("c (r w) -> c r w", w=SIDE),
                     src.rearrange("c (r w) -> c r w", w=ROW)[:, :, 0:SIDE])
                    for acc, src in zip((cA, cB), shifted)]

        @block.sync
        def _(sp):
            sp.dma_start(x_tile(0).rearrange("p (i f) -> p i f", i=2), x_d[0]).then_inc(s["x_loaded"], 16)
            sp.dma_start(cols[:, :], cols_d).then_inc(s["w0_loaded"], 16)
            sp.dma_start(ident[:, :], ident_d).then_inc(s["w0_loaded"], 16)
            sp.dma_start(w0[:, :], w0_d).then_inc(s["w0_loaded"], 16)
            sp.dma_start(rows[:, :], rows_d.broadcast_to([P, 3 * D])).then_inc(s["w0_loaded"], 16)
            sp.dma_start(mix[:, :].rearrange("p (k n) -> p k n", k=2),
                         mix_d.rearrange("(k p) n -> p k n", p=P)).then_inc(s["w0_loaded"], 16)
            sp.dma_start(w1[:, :], w1_d).then_inc(s["w1_loaded"], 16)
            for t in range(1, TILES):
                sp.wait_ge(s["x_loaded"], 16 * t)
                sp.dma_start(x_tile(t).rearrange("p (i f) -> p i f", i=2), x_d[t]).then_inc(s["x_loaded"], 16)
            with sp.Fori(0, TILES) as t:
                sp.wait_ge(s["y_ready"], t + 1)
                sp.dma_start(out_d[bass.ds(t, 1)].rearrange("t p i f -> (t p) i f"),
                             y[:, :].rearrange("p (i f) -> p i f", i=2)).then_inc(s["y_stored"], 16)
            sp.wait_ge(s["y_stored"], 16 * TILES)

        @block.gpsimd
        def _(pool):
            pool.memset(ones[:, :], 1.0).then_inc(s["ones_set"], 1)
            for constant, value in ((power, -0.5), (minus, -1.0), (eps0, EPS0), (eps1, EPS1)):
                pool.memset(constant[:, :], value).then_inc(s["ones_set"], 1)
            for zeroed in (pA, pB, woB0, woB1):
                pool.memset(zeroed[:, :], 0.0).then_inc(s["pads_zero"], 1)
            pool.wait_ge(s["ones_set"], 5)

            def split_low(lo, v, hi):
                return pool.tensor_tensor(lo[0:D, :], v[0:D, :], hi[0:D, :].bitcast(F32), ALU.subtract)

            def inverse_std(rs, mv, eps, step, done):
                pool.tensor_tensor(rs[:, :], mv[:, 1:8:2], eps[:, :], ALU.add).then_inc(step, 1)
                pool.wait_ge(step, done + 1)
                pool.tensor_tensor(rs[:, :], rs[:, :], power[:, :], ALU.pow).then_inc(step, 1)

            def minus_mean(ng, mv, step):
                pool.tensor_tensor(ng[:, :], mv[:, 0:8:2], minus[:, :], ALU.mult).then_inc(step, 1)

            def normalize(xn, v, ng, rs, ready):
                for k in range(CHUNKS):
                    pool.tensor_scalar(xn[:, k * D:(k + 1) * D], v[:, k * D:(k + 1) * D], ng[:, k:k + 1],
                                       rs[:, k:k + 1], ALU.add, ALU.mult).then_inc(ready, 1)

            def add_row(res, v, row, ready):
                pool.tensor_tensor(res.rearrange("p (k c) -> p k c", c=D),
                                   v.rearrange("p (k c) -> p k c", c=D),
                                   row.unsqueeze(1).broadcast_to([P, CHUNKS, D]), ALU.add).then_inc(ready, 1)

            def body0(i):
                n, f, c, m, g = i + 2, i + 1, i, i - 1, i - 2
                if tile_known(f):
                    pool.wait_ge(s["x1_split"], 2 * f + 2)
                    wait(pool, s["p_psum"], 2 * f)
                    split_low(xl1, xc1, xh1).then_inc(s["x1_lo"], 1)
                if tile_known(g):
                    add_row(x_tile(g), x2[:, :], rows[:, D:2 * D], s["x2b_ready"])
                if tile_known(n):
                    pool.wait_ge(s["mv1_ready"], 4 * n + 4)
                    wait(pool, s["xn1_ready"], 4 * n)
                    minus_mean(ng1, mv1, s["ln1_step"])
                    inverse_std(rs1, mv1, eps0, s["ln1_step"], 4 * n + 1)
                    pool.wait_ge(s["ln1_step"], 4 * n + 3)
                    pool.tensor_tensor(ng1[:, :], ng1[:, :], rs1[:, :], ALU.mult).then_inc(s["ln1_step"], 1)
                if tile_known(g):
                    pool.wait_ge(s["x2_split"], 2 * g + 2)
                    wait(pool, s["hid_psum"], 3 * g)
                    split_low(xl2, xc2, xh2).then_inc(s["x2_lo"], 1)
                if tile_known(m):
                    pool.wait_ge(s["mvm_ready"], 4 * m + 4)
                    inverse_std(rsm, mvm, eps0, s["lnm_step"], 2 * m)
                    pool.wait_ge(s["mv2_ready"], 4 * m + 4)
                    minus_mean(ng2, mv2, s["ln2_step"])
                    inverse_std(rs2, mv2, eps0, s["ln2_step"], 3 * m + 1)
                    wait(pool, s["tr2_done"], m)
                    pool.wait_ge(s["ln2_step"], 3 * m + 3)
                if tile_known(c):
                    pool.wait_ge(s["x_loaded"], 16 * c + 16)
                    if isinstance(i, int) and i == 0:
                        pool.wait_ge(s["prep"], PREP_BROW)
                    wait(pool, s["x2_ready"], 4 * c)
                    add_row(xb[:, :], x_tile(c), brow[:, :], s["xb_ready"])
                if tile_known(m):
                    normalize(xn2, x2, ng2, rs2, s["xn2_ready"])

            run0(pool, body0)

            def body1(i):
                n, f, m = i + 2, i + 1, i - 1
                if tile_known(m):
                    pool.wait_ge(s["mv4_ready"], 4 * m + 4)
                    wait(pool, s["xn4_ready"], 4 * m)
                    inverse_std(rs4, mv4, eps1, s["ln4_step"], 2 * m)
                if tile_known(n):
                    pool.wait_ge(s["mv3_ready"], 4 * n + 4)
                    wait(pool, s["xn3_ready"], 4 * n)
                    inverse_std(rs3, mv3, eps1, s["ln3_step"], 2 * n)
                if tile_known(f):
                    pool.wait_ge(s["x3_split"], 2 * f + 2)
                    wait(pool, s["ugv_psum"], 3 * f)
                    split_low(xl3, xc3, xh3).then_inc(s["x3_lo"], 1)
                if tile_known(m):
                    wait(pool, s["y_ready"], m)
                    add_row(x4b[:, :], x4[:, :], rows[:, 2 * D:3 * D], s["x4b_ready"])
                    pool.wait_ge(s["x4_split"], 2 * m + 2)
                    wait(pool, s["hid1_psum"], 3 * m)
                    split_low(xl4, xc4, xh4).then_inc(s["x4_lo"], 1)

            run1(pool, body1)

        @block.scalar
        def _(act):
            def split_high(xc, xh, src, done):
                act.activation(xc, src, ACT.Copy).then_inc(done, 1)
                act.activation(xh, src, ACT.Copy).then_inc(done, 1)

            def body0(i):
                n, f, m, g = i + 2, i + 1, i - 1, i - 2
                if tile_known(m):
                    for k in range(2):
                        if k == 0:
                            act.wait_ge(s["cT_done"], 2 * m + 2)
                            wait(act, s["mix_done"], 2 * m)
                        act.activation(local[:, k * 384:(k + 1) * 384], bank[4 + k][:, 0:384],
                                       ACT.Copy).then_inc(s["local_ready"], 1)
                if tile_known(f):
                    act.wait_ge(s["trx_done"], f + 1)
                    wait(act, s["x1_lo"], f)
                    wait(act, s["p_psum"], 2 * f)
                    split_high(xc1[0:D, :].rearrange("c (i p a) -> c i a p", i=2, a=2),
                               xh1[0:D, :].rearrange("c (i p a) -> c i a p", i=2, a=2),
                               bank[0][0:D, :].rearrange("c (i a p) -> c i a p", i=2, a=2), s["x1_split"])
                if tile_known(m):
                    wait(act, s["mtr_done"], m)
                    wait(act, s["mvm_ready"], 4 * m)
                    for a in range(2):
                        act.wait_ge(s["mix_done"], 2 * m + a + 1)
                        act.activation(mixed[:, a * 384:(a + 1) * 384], bank[4 + a][:, 0:384],
                                       ACT.Copy).then_inc(s["mixed_ready"], 1)
                if tile_known(g):
                    act.wait_ge(s["tr2_done"], g + 1)
                    wait(act, s["x2_lo"], g)
                    wait(act, s["hid_psum"], 3 * g)
                    split_high(xc2[0:D, :], xh2[0:D, :], bank[1][0:D, :], s["x2_split"])
                if tile_known(m):
                    act.wait_ge(s["mtr_done"], m + 1)
                    wait(act, s["wout_done"], m)
                    act.activation(mcA[:, :], bank[4][:, :], ACT.Copy).then_inc(s["mc_ready"], 1)
                    act.activation(mcB[:, :], bank[5][:, 0:TOKENS], ACT.Copy).then_inc(s["mc_ready"], 1)
                if tile_known(n):
                    act.wait_ge(s["ln1_step"], 4 * n + 4)
                    act.wait_ge(s["x_loaded"], 16 * n + 16)
                    wait(act, s["trx_done"], n)
                    xt = x_tile(n)
                    for k in range(CHUNKS):
                        act.activation(xn1[:, k * D:(k + 1) * D], xt[:, k * D:(k + 1) * D], ACT.Identity,
                                       bias=ng1[:, k:k + 1], scale=rs1[:, k:k + 1]).then_inc(s["xn1_ready"], 1)
                if tile_known(g):
                    wait(act, s["w2_done"], g)
                    for j in range(HJ):
                        act.wait_ge(s["hid_psum"], 3 * g + j + 1)
                        act.activation(hid[:, j * TILE:(j + 1) * TILE], bank[6 + j % 2][:, :], ACT.Gelu,
                                       bias=B[f"b1_{j}"]).then_inc(s["gelu_done"], 1)
                if tile_known(f):
                    act.wait_ge(s["p_psum"], 2 * f + 2)
                    if isinstance(i, int) and i == -1:
                        act.wait_ge(s["pads_zero"], 4)
                        act.wait_ge(s["prep"], PREP_BIAS0)
                    padded = (pA[:, LEAD:LEAD + 2 * IMG].rearrange("c (i r w) -> c i r w", i=2, w=ROW),
                              pB[:, LEAD:LEAD + IMG].rearrange("c (i r w) -> c i r w", i=1, w=ROW))
                    for grp, psum in enumerate((bank[2][:, :], bank[3][:, 0:TOKENS])):
                        acc, src = tap_views(0)[grp]
                        wait(act, s["conv_step"], 16 * f + grp - 1)
                        act.activation(padded[grp][:, :, 0:SIDE, 0:SIDE],
                                       psum.rearrange("c (i r w) -> c i r w", r=SIDE, w=SIDE),
                                       ACT.Identity, bias=B[("inA", "inB")[grp]]).then_inc(s["p_ready"], 1)
                        wait(act, s["cT_done"], 2 * f + grp - 1)
                        act.wait_ge(s["p_ready"], 2 * f + 1 + grp)
                        act.activation(acc, src, ACT.Copy, scale=col(("kA0", "kB0")[grp]))\
                           .then_inc(s["tap0_done"], 1)

            act.preload_act_table(ACT.Gelu)
            run0(act, body0)

            def body1(i):
                f, c, m, g = i + 1, i, i - 1, i - 2

                def seed(k):
                    if tile_known(c):
                        for h in range(2):
                            if k != 1:
                                wait(act, s["q_ready"], QS * c + (2 * k - 2 + h if k else h - 1))
                            act.activation(rec(k, h), vh[0:D, half(h)], ACT.Copy).then_inc(s["seeded"], 1)

                def gelu(j):
                    if tile_known(g):
                        if j == 0:
                            wait(act, s["m2_done"], g)
                        act.wait_ge(s["hid1_psum"], 3 * g + j + 1)
                        act.activation(hid1[:, j * TILE:(j + 1) * TILE], bank[M1_BANK[j]][:, :],
                                       ACT.Gelu_apprx_tanh, bias=B[f"m1_{j}"]).then_inc(s["gelu1_done"], 1)

                if tile_known(c):
                    if isinstance(i, int) and i == 0:
                        act.wait_ge(s["bits_set"], 4)
                    act.wait_ge(s["ugv_psum"], 3 * c + 1)
                    wait(act, s["seeded"], 14 * c)
                    act.activation(vh[0:D, :], bank[V_BANK][0:D, :], ACT.Identity,
                                   bias=B["v_half"][0:D]).then_inc(s["ugv_ready"], 1)
                    act.wait_ge(s["ugv_psum"], 3 * c + 2)
                    wait(act, s["q_ready"], QS * c)
                    act.activation(th[0:D, :], bank[G_BANK][0:D, :], ACT.Tanh, bias=B["g_half"][0:D],
                                   scale=0.5).then_inc(s["ugv_ready"], 1)
                    act.wait_ge(s["ugv_ready"], 3 * c + 1)
                seed(0)
                if tile_known(c):
                    act.wait_ge(s["ugv_psum"], 3 * c + 3)
                    wait(act, s["h8_ready"], c)
                    act.activation(nu[0:D, :], bank[U_BANK][0:D, :], ACT.Identity, bias=B["u_neg_half"][0:D],
                                   scale=-0.5).then_inc(s["ugv_ready"], 1)
                seed(1)
                gelu(0)
                gelu(1)
                seed(2)
                gelu(2)
                seed(3)
                if tile_known(f):
                    act.wait_ge(s["tr3_done"], f + 1)
                    wait(act, s["x3_lo"], f)
                    wait(act, s["ugv_psum"], 3 * f)
                    split_high(xc3[0:D, :], xh3[0:D, :], bank[4][0:D, :], s["x3_split"])
                seed(4)
                seed(5)
                if tile_known(m):
                    act.wait_ge(s["tr4_done"], m + 1)
                    wait(act, s["x4_lo"], m)
                    wait(act, s["hid1_psum"], 3 * m)
                    split_high(xc4[0:D, :], xh4[0:D, :], bank[4][0:D, :], s["x4_split"])
                seed(6)

            act.preload_act_table(ACT.Gelu_apprx_tanh)
            run1(act, body1)

        @block.vector
        def _(dve):
            def stats(st, mv, chunk, step, ready, t, between):
                for k in range(CHUNKS):
                    dve.bn_stats(st[:, 6 * k:6 * k + 6], chunk(k)).then_inc(step, 1)
                between(0)
                dve.wait_ge(step, 4 * t + 4)
                between(1)
                for k in range(CHUNKS):
                    dve.bn_aggr(mv[:, 2 * k:2 * k + 2], st[:, 6 * k:6 * k + 6]).then_inc(ready, 1)

            count = [0]

            def prep(instruction):
                count[0] += 1
                instruction.then_inc(s["prep"], 1)
                return count[0]

            def split_weight(v, hi, lo, width, done):
                dve.wait_ge(s["prep"], done)
                high = prep(dve.tensor_copy(hi[0:D, 0:width], v[0:D, 0:width]))
                dve.wait_ge(s["prep"], high)
                return prep(dve.tensor_tensor(lo[0:D, 0:width], v[0:D, 0:width],
                                              hi[0:D, 0:width].bitcast(F32), ALU.subtract))

            def w0s(name, n=P):
                return w0[0:n, W0[name][0]:W0[name][1]]

            def w1s(name, n=P):
                return w1[0:n, W1[name][0]:W1[name][1]]

            def scaled(res, v, factor, scale2=None):
                return prep(dve.tensor_scalar(res, v, factor, scale2, ALU.mult, ALU.bypass if scale2 is None else ALU.mult))

            def setup0():
                dve.wait_ge(s["w0_loaded"], 80)
                dve.wait_ge(s["ones_set"], 1)
                scaled(onbA[:, :], ones[:, :], col("on_bA"))
                scaled(onbB[:, :], ones[:, :], col("on_bB"))
                scaled(woA_f[:, :], w0s("w_outA"), col("on_gA"))
                done = scaled(woB_f[:, :], w0s("w_outB"), col("on_gB"))
                assert done == PREP_WOUT
                done = scaled(wi_f[0:D, :], w0s("w_in", D), col("n1_g", D))
                done = split_weight(wi_f, wi_h, wi_l, 384, done)
                assert done == PREP_WIN
                dve.wait_ge(s["prep_psum"], 1)
                for k, name in enumerate(("inA", "inB", "b1_0", "b1_1", "b1_2")):
                    done = prep(dve.tensor_tensor(B[name], bank[0][:, k:k + 1],
                                                  col({"inA": "b_inA", "inB": "b_inB"}.get(name, name)), ALU.add))
                assert done == PREP_BIAS0
                dve.wait_ge(s["prep_psum"], 2)
                done = prep(dve.tensor_tensor(brow[:, :], bank[1][:, 0:D], rows[:, 0:D], ALU.add))
                assert done == PREP_BROW
                dve.wait_ge(s["prep_psum"], 3)
                dve.wait_ge(s["pads_zero"], 4)
                for res, v, lo, hi in ((woA, woA_f, 0, P), (woB0, woB_f, 0, HB), (woB1, woB_f, HB, P)):
                    done = prep(dve.scalar_tensor_tensor(out=res[lo:hi, :], in0=bank[2][lo:hi, 0:D],
                                                         scalar=-1.0 / INNER, in1=v[lo:hi, :],
                                                         op0=ALU.mult, op1=ALU.add))
                assert done == PREP_WOC
                done = scaled(w1_f[0:D, :], w0s("w1", D), col("n2_g", D))
                done = split_weight(w1_f, w1_h, w1_l, 384, done)
                assert done == PREP_W1

            def setup1():
                dve.wait_ge(s["w1_loaded"], 16)
                prep(dve.tensor_tensor(a_i[0:D, :], w1s("A", D), ident[0:D, 0:D], ALU.subtract))
                done = scaled(a_half[0:D, :], w1s("A", D), 0.5)
                dve.wait_ge(s["prep_psum"], 4)
                done = prep(dve.tensor_copy(wuT[0:D, :], bank[4][0:D, 0:D]))
                assert done == PREP_WUT
                dve.wait_ge(s["prep_psum"], 5)
                bu = prep(dve.tensor_tensor(B["u"][0:D], bank[6][0:D, 0:1], col("bu", D), ALU.add))
                assert bu == PREP_BU
                bg = prep(dve.tensor_tensor(B["g_half"][0:D], bank[6][0:D, 1:2], col("bg", D), ALU.add))
                for j in range(HJ):
                    prep(dve.tensor_tensor(B[f"m1_{j}"], bank[6][:, 2 + j:3 + j], col(f"m1_{j}"), ALU.add))
                dve.wait_ge(s["prep"], bg)
                scaled(B["u_neg_half"][0:D], B["u"][0:D], -0.5)
                scaled(B["g_half"][0:D], B["g_half"][0:D], 0.5)
                scaled(w3_f[0:D, 0:2 * D], w1[0:D, 0:2 * D], col("s3", D))
                dve.wait_ge(s["prep_psum"], 6)
                done = scaled(w3_f[0:D, 2 * D:3 * D], bank[5][0:D, 0:D], col("s3", D), 0.5)
                split_weight(w3_f, w3_h, w3_l, 3 * D, done)
                dve.wait_ge(s["prep_psum"], 7)
                scaled(B["v_half"][0:D], bank[7][0:D, 0:1], 0.5)
                done = scaled(m1_f[0:D, :], w1s("m1", D), col("s4", D))
                done = split_weight(m1_f, m1_h, m1_l, 384, done)
                assert done == PREP_ALL

            def body0(i):
                n, c, m, e = i + 2, i, i - 1, i - 3

                def tap(k, groups=(0, 1)):
                    if not tile_known(c):
                        return
                    for grp in groups:
                        acc, src = tap_views(k)[grp]
                        if k == 1:
                            dve.wait_ge(s["tap0_done"], 2 * c + 1 + grp)
                        else:
                            dve.wait_ge(s["conv_step"], 16 * c + 2 * k - 3 + grp)
                        dve.scalar_tensor_tensor(out=acc, in0=src, scalar=col(f"k{'AB'[grp]}{k}"), in1=acc,
                                                 op0=ALU.mult, op1=ALU.add).then_inc(s["conv_step"], 1)

                if tile_known(n):
                    dve.wait_ge(s["x_loaded"], 16 * n + 16)
                    wait(dve, s["ln1_step"], 4 * n)
                    xt = x_tile(n)
                    stats(st1, mv1, lambda k: xt[:, k * D:(k + 1) * D], s["bn1_step"], s["mv1_ready"], n,
                          between=lambda grp: tap(1, [grp]))
                else:
                    tap(1)
                tap(2)
                tap(3)
                if tile_known(e):
                    dve.wait_ge(s["x2b_ready"], e + 1)
                    dve.wait_ge(s["w2_done"], e + 1)
                    dve.tensor_tensor(x_tile(e), bank[7][:, 0:384], x_tile(e), ALU.add).then_inc(s["x3_ready"], 1)
                tap(4)
                if tile_known(m):
                    dve.wait_ge(s["mixed_ready"], 2 * m + 2)
                    wait(dve, s["lnm_step"], 2 * m)
                    stats(stm, mvm, lambda k: mixed[:, (k % 2) * 384 + (k // 2) * INNER:(k % 2) * 384 + (k // 2 + 1) * INNER],
                          s["bnm_step"], s["mvm_ready"], m, between=lambda grp: tap(5, [grp]))
                else:
                    tap(5)
                tap(6)
                tap(7)
                if tile_known(m):
                    dve.wait_ge(s["xb_ready"], m + 1)
                    dve.wait_ge(s["lnm_step"], 2 * m + 2)
                    wait(dve, s["xn2_ready"], 4 * m)
                    wait(dve, s["x2b_ready"], m)
                    dve.wait_ge(s["wout_done"], m + 1)
                    for k in range(CHUNKS):
                        dve.scalar_tensor_tensor(out=x2[:, k * D:(k + 1) * D], in0=bank[1][:, k * D:(k + 1) * D],
                                                 scalar=rsm[:, k:k + 1], in1=xb[:, k * D:(k + 1) * D],
                                                 op0=ALU.mult, op1=ALU.add).then_inc(s["x2_ready"], 1)
                    wait(dve, s["ln2_step"], 3 * m)
                    dve.wait_ge(s["x2_ready"], 4 * m + 4)
                    stats(st2, mv2, lambda k: x2[:, k * D:(k + 1) * D], s["bn2_step"], s["mv2_ready"], m,
                          between=lambda grp: tap(8, [grp]))
                else:
                    tap(8)

            body0(-2)
            setup0()
            body0(-1)
            setup1()
            run(dve, body0, 0, 3, TILES - 2, TILES + 3)

            def body1(i):
                n, c, m, g = i + 2, i, i - 1, i - 2

                def step(k, halves=(0, 1)):
                    if tile_known(c):
                        for h in halves:
                            dve.wait_ge(s["step_done"], 14 * c + 2 * k + h + 1)
                            dve.scalar_tensor_tensor(out=q[0:D, half(h)], in0=th[0:D, half(h)], scalar=1.0,
                                                     in1=rec(k, h), op0=ALU.add, op1=ALU.mult)\
                               .then_inc(s["q_ready"], 1)

                def normalize(xn, v, mv, rs, ready):
                    for k in range(CHUNKS):
                        dve.tensor_scalar(xn[:, k * D:(k + 1) * D], v[:, k * D:(k + 1) * D],
                                          mv[:, 2 * k:2 * k + 1], rs[:, k:k + 1],
                                          ALU.subtract, ALU.mult).then_inc(ready, 1)

                if tile_known(c):
                    dve.wait_ge(s["ugv_ready"], 3 * c + 3)
                    dve.scalar_tensor_tensor(out=q[0:D, :], in0=th[0:D, :], scalar=1.0, in1=nu[0:D, :],
                                             op0=ALU.add, op1=ALU.mult).then_inc(s["q_ready"], 1)
                if tile_known(m):
                    dve.wait_ge(s["trh_done"], m + 1)
                    wait(dve, s["xn4_ready"], 4 * m)
                    wait(dve, s["x4b_ready"], m)
                    dve.tensor_tensor(x4[:, :], bank[4][:, 0:384], x_tile(m), ALU.add).then_inc(s["x4_ready"], 1)
                    wait(dve, s["ln4_step"], 2 * m)
                    dve.wait_ge(s["x4_ready"], m + 1)
                    stats(st4, mv4, lambda k: x4[:, k * D:(k + 1) * D], s["bn4_step"], s["mv4_ready"], m,
                          between=lambda h: step(0, [h]))
                else:
                    step(0)
                step(1)
                if tile_known(n):
                    dve.wait_ge(s["x3_ready"], n + 1)
                    wait(dve, s["ln3_step"], 2 * n)
                    wait(dve, s["xn3_ready"], 4 * n)
                    xt = x_tile(n)
                    stats(st3, mv3, lambda k: xt[:, k * D:(k + 1) * D], s["bn3_step"], s["mv3_ready"], n,
                          between=lambda h: step(2, [h]))
                else:
                    step(2)
                step(3)
                if tile_known(m):
                    dve.wait_ge(s["ln4_step"], 2 * m + 2)
                    wait(dve, s["tr4_done"], m)
                    normalize(xn4, x4, mv4, rs4, s["xn4_ready"])
                step(4)
                if tile_known(g):
                    dve.wait_ge(s["x4b_ready"], g + 1)
                    wait(dve, s["y_stored"], 16 * g)
                    dve.wait_ge(s["m2_done"], g + 1)
                    dve.tensor_tensor(y[:, :], bank[V_BANK][:, 0:384], x4b[:, :], ALU.add).then_inc(s["y_ready"], 1)
                step(5)
                if tile_known(n):
                    dve.wait_ge(s["ln3_step"], 2 * n + 2)
                    wait(dve, s["tr3_done"], n)
                    normalize(xn3, xt, mv3, rs3, s["xn3_ready"])
                step(6)
                if tile_known(c):
                    wait(dve, s["trh_done"], c)
                    dve.wait_ge(s["q_ready"], QS * c + QS)
                    dve.scalar_tensor_tensor(out=h8[0:D, :], in0=nu[0:D, :], scalar=-2.0, in1=q[0:D, :],
                                             op0=ALU.mult, op1=ALU.add).then_inc(s["h8_ready"], 1)

            run1(dve, body1)

        @block.tensor
        def _(pe):
            def wc0(name, lo=0, hi=None, n=P):
                a, b = W0[name]
                return w0[0:n, a + lo:b if hi is None else a + hi]

            def wc1(name, lo=0, hi=None, n=P):
                a, b = W1[name]
                return w1[0:n, a + lo:b if hi is None else a + hi]

            def setup0():
                pe.wait_ge(s["w0_loaded"], 80)
                pe.matmul(bank[0][:, 0:1], wc0("w_in", 0, 128, D), col("n1_b", D), start=True, stop=True)
                pe.matmul(bank[0][:, 1:2], wc0("w_in", 128, 256, D), col("n1_b", D), start=True, stop=False)
                pe.matmul(bank[0][:, 1:2], wc0("w_in", 256, 384, D), col("n1_b", D), start=False, stop=True)
                for j in range(HJ):
                    last = pe.matmul(bank[0][:, 2 + j:3 + j], wc0("w1", j * P, (j + 1) * P, D), col("n2_b", D),
                                     start=True, stop=True)
                last.then_inc(s["prep_psum"], 1)
                pe.wait_ge(s["prep"], PREP_WOUT)
                pe.matmul(bank[1][:, 0:D], onbA[:, :], wc0("w_outA"), start=True, stop=False)
                pe.matmul(bank[1][:, 0:D], onbB[0:HB, :], wc0("w_outB", n=HB), start=False, stop=True)\
                  .then_inc(s["prep_psum"], 1)
                pe.matmul(bank[2][:, 0:D], ones[:, :], woA_f[:, :], start=True, stop=False)
                pe.matmul(bank[2][:, 0:D], ones[0:HB, :], woB_f[0:HB, :], start=False, stop=True)\
                  .then_inc(s["prep_psum"], 1)

            def setup1():
                pe.wait_ge(s["w1_loaded"], 16)
                pe.transpose(bank[4][0:D, 0:D], wc1("Wu", n=D), ident[0:D, 0:D]).then_inc(s["prep_psum"], 1)
                pe.matmul(bank[6][0:D, 0:1], wc1("Wu", n=D), col("c3", D), start=True, stop=True)
                pe.matmul(bank[6][0:D, 1:2], wc1("Wg", n=D), col("c3", D), start=True, stop=True)
                for j in range(HJ):
                    last = pe.matmul(bank[6][:, 2 + j:3 + j], wc1("m1", j * P, (j + 1) * P, D), col("c4", D),
                                     start=True, stop=True)
                last.then_inc(s["prep_psum"], 1)
                pe.wait_ge(s["prep"], PREP_WUT)
                pe.matmul(bank[5][0:D, 0:D], wuT[0:D, :], a_i[0:D, :], start=True, stop=True).then_inc(s["prep_psum"], 1)
                pe.wait_ge(s["prep"], PREP_BU)
                pe.matmul(bank[7][0:D, 0:1], a_i[0:D, :], B["u"][0:D], start=True, stop=True).then_inc(s["prep_psum"], 1)

            def transposes(dst, src, done):
                for k in range(CHUNKS):
                    last = pe.transpose(dst[0:D, k * P:(k + 1) * P], src[:, k * D:(k + 1) * D], ident[:, :])
                last.then_inc(done, 1)

            def three_passes(dst, wh, wl, xh, xl, first=True, last=True):
                pe.matmul(dst, wh, xh, start=first, stop=False)
                pe.matmul(dst, wh, xl, start=False, stop=False)
                return pe.matmul(dst, wl, xh, start=False, stop=last)

            def body0(i):
                f, m, g, e = i + 1, i - 1, i - 2, i - 3
                if isinstance(i, int) and i == 1:
                    pe.wait_ge(s["prep"], PREP_ALL)
                def w1(j):
                    if tile_known(g):
                        if j == 1:
                            wait(pe, s["x3_ready"], g)
                        if j == 0:
                            pe.wait_ge(s["x2_lo"], g + 1)
                            pe.wait_ge(s["x2_split"], 2 * g + 2)
                        wait(pe, s["gelu_done"], 3 * g + max(j - 1, 0))
                        w = slice(P * j, P * (j + 1))
                        three_passes(bank[6 + j % 2][:, :], w1_h[0:D, w], w1_l[0:D, w], xh2[0:D, :], xl2[0:D, :])\
                            .then_inc(s["hid_psum"], 1)

                def w2(j):
                    if tile_known(e):
                        pe.wait_ge(s["gelu_done"], 3 * e + max(j + 1, 2))
                        for k in range(CHUNKS):
                            last = pe.matmul(bank[7][:, k * D:(k + 1) * D],
                                             hid[:, j * TILE + k * P:j * TILE + (k + 1) * P],
                                             wc0("w2", j * D, (j + 1) * D), start=(j == 0 and k == 0),
                                             stop=(j == HJ - 1), skip_group_check=True)
                        if j == HJ - 1:
                            last.then_inc(s["w2_done"], 1)

                w2(0)
                if tile_known(m):
                    wait(pe, s["mc_ready"], 2 * m)
                    for grp, parts in enumerate((((0, cA, 0), (2, cA, 2 * P + SIDE)), ((1, cB, 0),))):
                        pe.wait_ge(s["conv_step"], 16 * m + 15 + grp)
                        for k in range(2):
                            for part, acc, at in parts:
                                last = pe.transpose(bank[4 + k][:, part * P:(part + 1) * P],
                                                    acc[:, at + k * P:at + (k + 1) * P], ident[:, :])
                        last.then_inc(s["cT_done"], 1)
                if tile_known(f):
                    pe.wait_ge(s["xn1_ready"], 4 * f + 4)
                    wait(pe, s["x1_split"], 2 * f)
                    if isinstance(i, int) and i == -1:
                        pe.wait_ge(s["prep"], PREP_BIAS0)
                    transposes(bank[0], xn1, s["trx_done"])
                w2(1)
                w2(2)
                if tile_known(m):
                    pe.wait_ge(s["local_ready"], 2 * m + 2)
                    for a in range(2):
                        for k in range(2):
                            last = pe.matmul(bank[4 + a][:, 0:384],
                                             mix[:, k * TOKENS + a * P:k * TOKENS + (a + 1) * P],
                                             local[:, k * 384:(k + 1) * 384], start=(k == 0), stop=(k == 1))
                        last.then_inc(s["mix_done"], 1)
                if tile_known(g):
                    pe.wait_ge(s["xn2_ready"], 4 * g + 4)
                    pe.wait_ge(s["x2_ready"], 4 * g + 4)
                    transposes(bank[1], xn2, s["tr2_done"])
                if tile_known(m):
                    pe.wait_ge(s["mixed_ready"], 2 * m + 2)
                    for im in range(2):
                        for a in range(2):
                            src = mixed[:, a * 384 + 2 * P * im:a * 384 + 2 * P * im + P]
                            k = 2 * im + a
                            pe.transpose(bank[4][:, k * P:(k + 1) * P], src, ident[:, :])
                    for a in range(2):
                        last = pe.transpose(bank[5][:, a * P:(a + 1) * P], mixed[:, a * 384 + P:a * 384 + 2 * P],
                                            ident[:, :])
                    last.then_inc(s["mtr_done"], 1)
                if tile_known(f):
                    pe.wait_ge(s["x1_lo"], f + 1)
                    pe.wait_ge(s["x1_split"], 2 * f + 2)
                    if isinstance(i, int) and i == -1:
                        pe.wait_ge(s["prep"], PREP_WOC)
                    wait(pe, s["p_ready"], 2 * f)
                    three_passes(bank[2][:, :], wi_h[0:D, 0:P], wi_l[0:D, 0:P], xh1[0:D, :], xl1[0:D, :])\
                        .then_inc(s["p_psum"], 1)
                    for im in range(2):
                        w = slice(P * (im + 1), P * (im + 2))
                        x_ = slice(TOKENS * im, TOKENS * (im + 1))
                        last = three_passes(bank[3][:, 0:TOKENS], wi_h[0:D, w], wi_l[0:D, w], xh1[0:D, x_],
                                            xl1[0:D, x_], first=(im == 0), last=(im == 1))
                    last.then_inc(s["p_psum"], 1)
                if tile_known(m):
                    pe.wait_ge(s["mc_ready"], 2 * m + 2)
                    wait(pe, s["x2_split"], 2 * m)
                    for k in range(CHUNKS):
                        im, a = k // 2, k % 2
                        pe.matmul(bank[1][:, k * D:(k + 1) * D], mcA[:, k * P:(k + 1) * P], woA[:, :],
                                  start=True, stop=False)
                        last = pe.matmul(bank[1][:, k * D:(k + 1) * D], mcB[:, a * P:(a + 1) * P],
                                         (woB0, woB1)[im][:, :], start=False, stop=True)
                    last.then_inc(s["wout_done"], 1)
                w1(0)
                w1(1)
                w1(2)

            setup0()
            body0(-2)
            body0(-1)
            setup1()
            run(pe, body0, 0, 3, TILES - 2, TILES + 3)

            pe.wait_ge(s["x3_ready"], TILES)
            pe.wait_ge(s["p_ready"], 2 * TILES)
            for k in range(2):
                for h in range(2):
                    pe.matmul(rec(k, h), a_half[0:D, :], xc1[0:D, half(h)], start=True, stop=True)\
                      .then_inc(s["bits_set"], 1)

            def body1(i):
                f, c, m, g = i + 1, i, i - 1, i - 2

                def step(k):
                    if tile_known(c):
                        for h in range(2):
                            pe.wait_ge(s["seeded"], 14 * c + 2 * k + h + 1)
                            pe.wait_ge(s["q_ready"], QS * c + max(2 * k + h, 1))
                            pe.matmul(rec(k, h), a_half[0:D, :], q[0:D, half(h)], start=False, stop=True,
                                      skip_group_check=True).then_inc(s["step_done"], 1)

                def ugv(k):
                    if tile_known(f):
                        if k == 0:
                            pe.wait_ge(s["x3_lo"], f + 1)
                            pe.wait_ge(s["x3_split"], 2 * f + 2)
                            wait(pe, s["y_ready"], f - 2)
                        w = slice((2, 1, 0)[k] * D, ((2, 1, 0)[k] + 1) * D)
                        three_passes(bank[(V_BANK, G_BANK, U_BANK)[k]][0:D, :], w3_h[0:D, w], w3_l[0:D, w],
                                     xh3[0:D, :], xl3[0:D, :]).then_inc(s["ugv_psum"], 1)

                def m1(j):
                    if tile_known(g):
                        if j == 0:
                            pe.wait_ge(s["x4_lo"], g + 1)
                            pe.wait_ge(s["x4_split"], 2 * g + 2)
                        if tile_known(c):
                            pe.wait_ge(s["ugv_ready"], 3 * c + j + 1)
                        elif j == 0:
                            pe.wait_ge(s["y_ready"], g)
                        w = slice(P * j, P * (j + 1))
                        three_passes(bank[M1_BANK[j]][:, :], m1_h[0:D, w], m1_l[0:D, w], xh4[0:D, :], xl4[0:D, :])\
                            .then_inc(s["hid1_psum"], 1)

                def m2(j):
                    if tile_known(g):
                        pe.wait_ge(s["gelu1_done"], 3 * g + j + 1)
                        for k in range(CHUNKS):
                            last = pe.matmul(bank[V_BANK][:, k * D:(k + 1) * D],
                                             hid1[:, j * TILE + k * P:j * TILE + (k + 1) * P],
                                             wc1("m2", j * D, (j + 1) * D), start=(j == 0 and k == 0),
                                             stop=(j == HJ - 1), skip_group_check=True)
                        if j == HJ - 1:
                            last.then_inc(s["m2_done"], 1)

                if tile_known(m):
                    pe.wait_ge(s["h8_ready"], m + 1)
                    wait(pe, s["x4_split"], 2 * m)
                    for k in range(CHUNKS):
                        last = pe.transpose(bank[4][:, k * D:(k + 1) * D], h8[0:D, k * P:(k + 1) * P],
                                            ident[0:D, 0:D])
                    last.then_inc(s["trh_done"], 1)
                m1(0)
                m1(1)
                step(0)
                m1(2)
                step(1)
                if tile_known(f):
                    pe.wait_ge(s["xn3_ready"], 4 * f + 4)
                    wait(pe, s["x4_ready"], f - 1)
                    transposes(bank[4], xn3, s["tr3_done"])
                m2(0)
                step(2)
                m2(1)
                step(3)
                m2(2)
                step(4)
                if tile_known(m):
                    pe.wait_ge(s["xn4_ready"], 4 * m + 4)
                    pe.wait_ge(s["x4_ready"], m + 1)
                    if tile_known(f):
                        pe.wait_ge(s["x3_split"], 2 * f + 2)
                    transposes(bank[4], xn4, s["tr4_done"])
                step(5)
                ugv(0)
                step(6)
                ugv(1)
                ugv(2)

            run1(pe, body1)


QS = 2 * STEPS - 1
V_BANK, G_BANK, U_BANK = M1_BANK = 7, 5, 6

PREP_WOUT = 4
PREP_WIN = 7
PREP_BIAS0 = 12
PREP_BROW = 13
PREP_WOC = 16
PREP_W1 = 19
PREP_WUT = 22
PREP_BU = 23
PREP_ALL = 37


VECTORS = {
    "n1_g": "L0_conv_n1_g", "n1_b": "L0_conv_n1_b", "n2_g": "L0_conv_n2_g", "n2_b": "L0_conv_n2_b",
    "s3": "L1_conv_norm1_scale", "c3": "L1_conv_norm1_bias", "bu": "L1_conv_bu", "bg": "L1_conv_bg",
    "s4": "L1_conv_norm2_scale", "c4": "L1_conv_norm2_bias"}


def kernel(**inputs):
    import numpy as np
    import concourse.bacc as bacc
    from concourse.bass_utils import run_bass_kernel_spmd

    a = {k: np.asarray(v) for k, v in inputs.items()}
    cols = np.zeros((P, len(COLS)), np.float32)

    def put(name, v):
        cols[:len(v), COLS.index(name)] = v

    def put_inner(name, v):
        k = {"k": lambda g: name.replace("?", g)}["k"]
        put(k("A"), v[:P])
        put(k("B"), np.concatenate([v[P:], v[P:]]))

    for name, source in VECTORS.items():
        put(name, a[source])
    put_inner("b_in?", a["L0_conv_b_in"])
    put_inner("on_g?", a["L0_conv_on_g"])
    put_inner("on_b?", a["L0_conv_on_b"])
    taps = a["L0_conv_k_conv"].reshape(9, INNER)
    for t in range(9):
        put_inner(f"k?{t}", taps[t])
    for j in range(HJ):
        put(f"b1_{j}", a["L0_conv_b1"][j * P:(j + 1) * P])
        put(f"m1_{j}", a["L1_conv_mlp_b1"][j * P:(j + 1) * P])
    rows = np.concatenate([a["L0_conv_b_out"], a["L0_conv_b2"], a["L1_conv_mlp_b2"]])[None, :]

    w0 = np.zeros((P, 1248), np.float32)
    w0[:D, 0:P] = a["L0_conv_w_in"][:, :P]
    w0[:D, P:P + HB] = a["L0_conv_w_in"][:, P:]
    w0[:D, 2 * P + HB:3 * P] = a["L0_conv_w_in"][:, P:]
    w0[:, 384:480] = a["L0_conv_w_out"][:P]
    w0[:, 480:576] = np.concatenate([a["L0_conv_w_out"][P:]] * 2)
    w0[:D, 576:960] = a["L0_conv_w1"]
    w0[:, 960:1248] = a["L0_conv_w2"].reshape(HJ, P, D).transpose(1, 0, 2).reshape(P, HJ * D)
    w1 = np.zeros((P, 960), np.float32)
    w1[:D, 0:96] = a["L1_conv_Wu"]
    w1[:D, 96:192] = a["L1_conv_Wg"]
    w1[:D, 192:288] = a["L1_conv_A"]
    w1[:D, 288:672] = a["L1_conv_mlp_w1"]
    w1[:, 672:960] = a["L1_conv_mlp_w2"].reshape(HJ, P, D).transpose(1, 0, 2).reshape(P, HJ * D)

    at = np.arange(SIDE)
    both_ways = GAIN * DECAY ** np.abs(at[:, None] - at[None, :]) * (1 + (at[:, None] == at[None, :]))
    eye = np.eye(SIDE)
    mix = np.eye(TOKENS) + 0.25 * (np.kron(eye, both_ways) + np.kron(both_ways, eye))
    mix = mix.reshape(TOKENS, P, 2).transpose(0, 2, 1).reshape(TOKENS, TOKENS).astype(np.float32)

    arrays = {"x": np.ascontiguousarray(a["x"].reshape(IMAGES * P, 2 * D)), "cols": cols, "rows": rows, "w0": w0,
              "w1": w1, "mix": mix, "ident": np.eye(P, dtype=np.float32)}
    nc = bacc.Bacc("TRN2", target_bir_lowering=False, num_devices=1)
    args = [nc.dram_tensor(f"in_{n}", v.shape, F32, kind="ExternalInput").ap() for n, v in arrays.items()]
    out = nc.dram_tensor("out", (IMAGES * P, 2 * D), F32, kind="ExternalOutput").ap()
    build(nc, *args, out)
    r = run_bass_kernel_spmd(nc, [{f"in_{n}": v for n, v in arrays.items()}], core_ids=[0])
    return r.results[0]["out"].reshape(IMAGES, SIDE, SIDE, D)
```

```python
from contextlib import ExitStack

import concourse.bass as bass
from concourse import mybir

F32 = mybir.dt.float32
F32R = mybir.dt.float32r
ALU = mybir.AluOpType
ACT = mybir.ActivationFunctionType

IMAGES, SIDE, D = 16, 16, 96
INNER, HIDDEN, STEPS = 2 * D, 4 * D, 8
DECAY, GAIN = 0.6, 0.4
P = 128
TOKENS = SIDE * SIDE
TILES = IMAGES // 2
TILE = 2 * TOKENS
CHUNKS = TILE // P
HB = INNER - P
HJ = HIDDEN // P
ROW = SIDE + 1
IMG = ROW * ROW
LEAD = ROW + 1
TAPS = [(dy, dx) for dy in (-1, 0, 1) for dx in (-1, 0, 1)]
EPS0, EPS1 = 1e-5, 1e-6
QS = 2 * STEPS - 1
SEEDS = 2 * (STEPS - 1)

T_BANK = 0
V_BANK = 6
M1_BANK = (V_BANK, 7, 1)
REC_BANK = (4, 2, 5, 3)

PREP_WIN = 3
PREP_WOUT = 7
PREP_BIAS0 = 12
PREP_BROW = 13
PREP_WOC = 16
PREP_W1 = 19
PREP_WUT = 22
PREP_BU = 23
PREP_BG = 24
PREP_ALL = PREP_BG + HJ

COLS = (["n1_g", "n1_b", "b_inA", "b_inB"] + [f"kA{t}" for t in range(9)] + [f"kB{t}" for t in range(9)]
        + ["on_gA", "on_gB", "on_bA", "on_bB", "n2_g", "n2_b", "b1_0", "b1_1", "b1_2",
           "s3", "c3", "bu", "bg", "s4", "c4", "m1_0", "m1_1", "m1_2"])
W0 = {"w_in": (0, 384), "w_outA": (384, 480), "w_outB": (480, 576), "w1": (576, 960), "w2": (960, 1248)}
W0_EARLY = 576
W1 = {"Wu": (0, 96), "Wg": (96, 192), "A": (192, 288), "m1": (288, 672), "m2": (672, 960)}


def tile_known(t):
    return not isinstance(t, int) or 0 <= t < TILES


def peeled(i, k):
    return isinstance(i, int) and i == k


def is_last(t):
    return peeled(t, TILES - 1)


def wait(engine, sem, count):
    if not isinstance(count, int) or count > 0:
        engine.wait_ge(sem, count)


def build(nc, x, cols_d, rows_d, w0_d, w1_d, mix_d, ident_d, out):
    x_d = x.rearrange("(t i p) f -> t p i f", i=2, p=P)
    out_d = out.rearrange("(t i p) f -> t p i f", i=2, p=P)

    with ExitStack() as ctx:
        def sb(name, cols, dt=F32, rows=P):
            return ctx.enter_context(nc.sbuf_tensor(name, [rows, cols], dt))

        def sem(name):
            return ctx.enter_context(nc.semaphore(name))

        bank = [ctx.enter_context(nc.psum_tensor(f"bank{b}", [P, 512], F32)) for b in range(8)]

        cols = sb("cols", len(COLS))
        rows = sb("rows", 3 * D)
        w0 = sb("w0", 1248)
        w1 = sb("w1", 960)
        mix = sb("mix", 2 * TOKENS)
        ident = sb("ident", P)
        ones = sb("ones", P)
        onbA, onbB = sb("onbA", P), sb("onbB", P)
        wi_f, w1_f, m1_f, w3_f = sb("wi_f", 384), sb("w1_f", 384), sb("m1_f", 384), sb("w3_f", 288)
        wi_h, w1_h, m1_h, w3_h = (sb(n, c, F32R) for n, c in (
            ("wi_h", 384), ("w1_h", 384), ("m1_h", 384), ("w3_h", 288)))
        wi_l, w1_l, m1_l, w3_l = (sb(n, c, F32R) for n, c in (
            ("wi_l", 384), ("w1_l", 384), ("m1_l", 384), ("w3_l", 288)))
        woA_f, woB_f = sb("woA_f", D), sb("woB_f", D)
        woA, woB0, woB1 = sb("woA", D), sb("woB0", D), sb("woB1", D)
        a_i, a_half, wuT, wuai = sb("a_i", D), sb("a_half", D), sb("wuT", D), sb("wuai", D)
        bias = sb("bias", 16)
        brow = sb("brow", D)
        B = {n: bias[:, k:k + 1] for k, n in enumerate(
            ["inA", "inB", "b1_0", "b1_1", "b1_2", "m1_0", "m1_1", "m1_2", "u", "g", "u_neg_half", "g_half",
             "v_half"])}

        def col(name, n=P):
            k = COLS.index(name)
            return cols[0:n, k:k + 1]

        x_all = sb("x_all", TILES * CHUNKS * D)
        st1, mv1, rs1, ng1 = sb("st1", 24), sb("mv1", 8), sb("rs1", 4), sb("ng1", 4)
        st2, mv2, rs2, ng2 = sb("st2", 24), sb("mv2", 8), sb("rs2", 4), sb("ng2", 4)
        stm, mvm, rsm = sb("stm", 24), sb("mvm", 8), sb("rsm", 4)
        st3, mv3, rs3 = sb("st3", 24), sb("mv3", 8), sb("rs3", 4)
        st4, mv4, rs4 = sb("st4", 24), sb("mv4", 8), sb("rs4", 4)
        power, minus, eps0, eps1 = (sb(n, 4) for n in ("power", "minus", "eps0", "eps1"))
        xn1, xn2, xn3, xn4 = (sb(f"xn{k}", CHUNKS * D) for k in (1, 2, 3, 4))
        xc1, xc2, xc3, xc4 = (sb(f"xc{k}", TILE) for k in (1, 2, 3, 4))
        xh1, xh2, xh3, xh4 = (sb(f"xh{k}", TILE, F32R) for k in (1, 2, 3, 4))
        xl1, xl2, xl3, xl4 = (sb(f"xl{k}", TILE, F32R) for k in (1, 2, 3, 4))
        SPAN_A, SPAN_B = LEAD + 2 * IMG + LEAD, LEAD + IMG + LEAD
        pA, pB = sb("pA", SPAN_A), sb("pB", SPAN_B)
        cA, cB = sb("cA", (2 * SIDE + 1) * SIDE), sb("cB", TOKENS)
        local = sb("local", 2 * 2 * INNER)
        mixed = sb("mixed", 2 * 2 * INNER)
        mcA, mcB = sb("mcA", TILE), sb("mcB", TOKENS)
        xb, x2 = sb("xb", CHUNKS * D), sb("x2", CHUNKS * D)
        hid = sb("hid", HJ * TILE)
        th, nu, vh, q, h8 = (sb(n, TILE) for n in ("th", "nu", "vh", "q", "h8"))
        x4, x4b, y = sb("x4", CHUNKS * D), sb("x4b", CHUNKS * D), sb("y", CHUNKS * D)
        hid1 = sb("hid1", HJ * TILE)

        s = {n: sem(n) for n in (
            "cols_loaded", "ident_loaded", "rows_loaded", "w0_loaded", "w0_rest_loaded", "mix_loaded",
            "w1_loaded", "ones_set", "pads_zero", "prep", "prep_psum", "prep_high", "prep_low",
            "x_loaded", "bn1_step", "mv1_ready", "ln1_step", "xn1_ready", "trx_done", "x1_split", "x1_lo",
            "p_psum", "p_ready", "tap0_done", "conv_step", "cT_done", "local_ready", "mix_done", "mixed_ready",
            "bnm_step", "mvm_ready", "lnm_step", "mtr_done", "mc_ready", "wout_done", "xb_ready", "x2_ready",
            "bn2_step", "mv2_ready", "ln2_step", "xn2_ready", "x2b_ready", "tr2_done", "x2_split", "x2_lo",
            "hid_psum", "gelu_done", "w2_done", "x3_ready",
            "bn3_step", "mv3_ready", "ln3_step", "xn3_ready", "tr3_done", "x3_split", "x3_lo", "ugv_psum",
            "ugv_ready", "bits_set", "seeded", "step_done", "q_ready", "h8_ready", "trh_done", "x4_ready",
            "bn4_step", "mv4_ready", "ln4_step", "xn4_ready", "x4b_ready", "tr4_done", "x4_split", "x4_lo",
            "hid1_psum", "gelu1_done", "m2_done", "y_ready", "y_stored")}

        block = ctx.enter_context(nc.Block())

        def x_tile(t):
            return x_all[:, bass.ts(t, CHUNKS * D)]

        def half(h):
            return slice(h * TOKENS, (h + 1) * TOKENS)

        def rec(k, h):
            return bank[REC_BANK[2 * h + k % 2]][0:D, 0:TOKENS]

        def run(engine, body0, body1, turn, head=lambda i: None):
            for i in range(-2, 3):
                body0(i)
            with engine.Fori(3, TILES - 2) as i:
                body0(i)
            for i in range(TILES - 2, TILES + 1):
                body0(i)
                head(i)
            turn()
            body1(1)
            body1(2)
            with engine.Fori(3, TILES - 2) as i:
                body1(i)
            for i in range(TILES - 2, TILES + 2):
                body1(i)

        def vgu_bank(t):
            return (2, 3, T_BANK) if peeled(t, 0) else M1_BANK

        def tap_views(k):
            dy, dx = TAPS[k]
            at = LEAD + dy * ROW + dx
            shifted = (pA[:, at:at + (2 * SIDE + 1) * ROW], pB[:, at:at + SIDE * ROW])
            return [(acc[:, :].rearrange("c (r w) -> c r w", w=SIDE),
                     src.rearrange("c (r w) -> c r w", w=ROW)[:, :, 0:SIDE])
                    for acc, src in zip((cA, cB), shifted)]

        @block.sync
        def _(sp):
            sp.dma_start(x_tile(0).rearrange("p (i f) -> p i f", i=2), x_d[0]).then_inc(s["x_loaded"], 16)
            sp.dma_start(w0[:, 0:W0_EARLY], w0_d[:, 0:W0_EARLY]).then_inc(s["w0_loaded"], 16)
            sp.dma_start(w0[:, W0_EARLY:], w0_d[:, W0_EARLY:]).then_inc(s["w0_rest_loaded"], 16)

            def load_x(t):
                sp.wait_ge(s["x_loaded"], 16 * t)
                sp.dma_start(x_tile(t).rearrange("p (i f) -> p i f", i=2), x_d[t]).then_inc(s["x_loaded"], 16)

            load_x(1)
            sp.dma_start(mix[:, :].rearrange("p (k n) -> p k n", k=2),
                         mix_d.rearrange("(k p) n -> p k n", p=P)).then_inc(s["mix_loaded"], 16)
            load_x(2)
            sp.dma_start(w1[:, :], w1_d).then_inc(s["w1_loaded"], 16)
            for t in range(3, TILES):
                load_x(t)
            with sp.Fori(0, TILES) as t:
                sp.wait_ge(s["y_ready"], t + 1)
                sp.dma_start(out_d[bass.ds(t, 1)].rearrange("t p i f -> (t p) i f"),
                             y[:, :].rearrange("p (i f) -> p i f", i=2)).then_inc(s["y_stored"], 16)
            sp.wait_ge(s["y_stored"], 16 * TILES)

        @block.gpsimd
        def _(pool):
            pool.memset(ones[:, :], 1.0).then_inc(s["ones_set"], 1)
            for constant, value in ((power, -0.5), (minus, -1.0), (eps0, EPS0), (eps1, EPS1)):
                pool.memset(constant[:, :], value).then_inc(s["ones_set"], 1)
            for zeroed in (pA, pB, woB0, woB1):
                pool.memset(zeroed[:, :], 0.0).then_inc(s["pads_zero"], 1)
            pool.wait_ge(s["ones_set"], 5)

            def split_low(lo, v, hi):
                return pool.tensor_tensor(lo[0:D, :], v[0:D, :], hi[0:D, :].bitcast(F32), ALU.subtract)

            def inverse_std(rs, mv, eps, step, done):
                pool.tensor_tensor(rs[:, :], mv[:, 1:8:2], eps[:, :], ALU.add).then_inc(step, 1)
                pool.wait_ge(step, done + 1)
                pool.tensor_tensor(rs[:, :], rs[:, :], power[:, :], ALU.pow).then_inc(step, 1)

            def minus_mean(ng, mv, step):
                pool.tensor_tensor(ng[:, :], mv[:, 0:8:2], minus[:, :], ALU.mult).then_inc(step, 1)

            def normalize(xn, v, ng, rs, ready):
                for k in range(CHUNKS):
                    pool.tensor_scalar(xn[:, k * D:(k + 1) * D], v[:, k * D:(k + 1) * D], ng[:, k:k + 1],
                                       rs[:, k:k + 1], ALU.add, ALU.mult).then_inc(ready, 1)

            def add_row(res, v, row, ready):
                pool.tensor_tensor(res.rearrange("p (k c) -> p k c", c=D),
                                   v.rearrange("p (k c) -> p k c", c=D),
                                   row.unsqueeze(1).broadcast_to([P, CHUNKS, D]), ALU.add).then_inc(ready, 1)

            def setup2():
                for count, low, v, high in ((8, w3_l, w3_f, w3_h), (9, m1_l, m1_f, m1_h)):
                    pool.wait_ge(s["prep_high"], count)
                    pool.tensor_tensor(low[0:D, :], v[0:D, :], high[0:D, :].bitcast(F32), ALU.subtract)\
                        .then_inc(s["prep_low"], 1)

            def body0(i):
                n, f, c, m, g = i + 2, i + 1, i, i - 1, i - 2
                if tile_known(f):
                    pool.wait_ge(s["x1_split"], 2 * f + 2)
                    wait(pool, s["p_psum"], 2 * f)
                    split_low(xl1, xc1, xh1).then_inc(s["x1_lo"], 1)
                if tile_known(g):
                    add_row(x_tile(g), x2[:, :], rows[:, D:2 * D], s["x2b_ready"])
                if tile_known(n):
                    pool.wait_ge(s["mv1_ready"], 4 * n + 4)
                    wait(pool, s["xn1_ready"], 4 * n)
                    minus_mean(ng1, mv1, s["ln1_step"])
                    inverse_std(rs1, mv1, eps0, s["ln1_step"], 4 * n + 1)
                    pool.wait_ge(s["ln1_step"], 4 * n + 3)
                    pool.tensor_tensor(ng1[:, :], ng1[:, :], rs1[:, :], ALU.mult).then_inc(s["ln1_step"], 1)
                if tile_known(g):
                    pool.wait_ge(s["x2_split"], 2 * g + 2)
                    wait(pool, s["hid_psum"], 3 * g)
                    split_low(xl2, xc2, xh2).then_inc(s["x2_lo"], 1)
                if tile_known(m):
                    pool.wait_ge(s["mvm_ready"], 4 * m + 4)
                    inverse_std(rsm, mvm, eps0, s["lnm_step"], 2 * m)
                    if peeled(i, 1):
                        setup2()
                    pool.wait_ge(s["mv2_ready"], 4 * m + 4)
                    minus_mean(ng2, mv2, s["ln2_step"])
                    inverse_std(rs2, mv2, eps0, s["ln2_step"], 3 * m + 1)
                    wait(pool, s["tr2_done"], m)
                    pool.wait_ge(s["ln2_step"], 3 * m + 3)
                if tile_known(c):
                    pool.wait_ge(s["x_loaded"], 16 * c + 16)
                    if peeled(i, 0):
                        pool.wait_ge(s["prep"], PREP_BROW)
                    wait(pool, s["x2_ready"], 4 * c)
                    add_row(xb[:, :], x_tile(c), brow[:, :], s["xb_ready"])
                if tile_known(m):
                    normalize(xn2, x2, ng2, rs2, s["xn2_ready"])

            def ln3_std(n):
                if tile_known(n):
                    pool.wait_ge(s["mv3_ready"], 4 * n + 4)
                    wait(pool, s["xn3_ready"], 4 * n)
                    inverse_std(rs3, mv3, eps1, s["ln3_step"], 2 * n)

            def ln3_low(f):
                if tile_known(f):
                    pool.wait_ge(s["x3_split"], 2 * f + 2)
                    wait(pool, s["ugv_psum"], 3 * f)
                    split_low(xl3, xc3, xh3).then_inc(s["x3_lo"], 1)

            def head(i):
                if i == TILES - 2:
                    ln3_std(0)
                if i == TILES - 1:
                    ln3_low(0)
                    ln3_std(1)

            def turn():
                body0(TILES + 1)
                ln3_low(1)
                ln3_std(2)

            def body1(i):
                n, f, m = i + 2, i + 1, i - 1
                if tile_known(m):
                    pool.wait_ge(s["mv4_ready"], 4 * m + 4)
                    wait(pool, s["xn4_ready"], 4 * m)
                    inverse_std(rs4, mv4, eps1, s["ln4_step"], 2 * m)
                ln3_std(n)
                ln3_low(f)
                if tile_known(m):
                    wait(pool, s["y_ready"], m)
                    add_row(x4b[:, :], x4[:, :], rows[:, 2 * D:3 * D], s["x4b_ready"])
                if tile_known(m) and not is_last(m):
                    pool.wait_ge(s["x4_split"], 2 * m + 2)
                    wait(pool, s["hid1_psum"], 3 * m)
                    split_low(xl4, xc4, xh4).then_inc(s["x4_lo"], 1)

            run(pool, body0, body1, turn, head)

        @block.scalar
        def _(act):
            act.dma_start(cols[:, :], cols_d).then_inc(s["cols_loaded"], 16)
            act.dma_start(ident[:, :], ident_d).then_inc(s["ident_loaded"], 16)
            act.dma_start(rows[:, :], rows_d.broadcast_to([P, 3 * D])).then_inc(s["rows_loaded"], 16)

            def split_high(xc, xh, src, done):
                act.activation(xc, src, ACT.Copy).then_inc(done, 1)
                act.activation(xh, src, ACT.Copy).then_inc(done, 1)

            def setup2():
                act.wait_ge(s["prep"], PREP_BG)
                for name, source, scale in (("u_neg_half", "u", -0.5), ("g_half", "g", 0.5)):
                    act.activation(B[name][0:D], B[source][0:D], ACT.Copy, scale=scale)\
                       .then_inc(s["prep_high"], 1)
                act.wait_ge(s["w1_loaded"], 16)
                act.wait_ge(s["prep_psum"], 6)
                act.activation(B["v_half"][0:D], bank[7][0:D, 2 * P:2 * P + 1], ACT.Copy, scale=0.5)\
                   .then_inc(s["prep_high"], 1)
                act.activation(w3_f[0:D, 0:2 * D], w1[0:D, 0:2 * D], ACT.Copy, scale=col("s3", D))\
                   .then_inc(s["prep_high"], 1)
                act.activation(wuai[0:D, :], bank[7][0:D, P:P + D], ACT.Copy, scale=0.5)\
                   .then_inc(s["prep_high"], 1)
                act.activation(m1_f[0:D, :], w1[0:D, W1["m1"][0]:W1["m1"][1]], ACT.Copy, scale=col("s4", D))\
                   .then_inc(s["prep_high"], 1)
                act.wait_ge(s["prep_high"], 5)
                act.activation(w3_f[0:D, 2 * D:3 * D], wuai[0:D, :], ACT.Copy, scale=col("s3", D))\
                   .then_inc(s["prep_high"], 1)
                act.wait_ge(s["prep_high"], 7)
                act.activation(w3_h[0:D, :], w3_f[0:D, :], ACT.Copy).then_inc(s["prep_high"], 1)
                act.activation(m1_h[0:D, :], m1_f[0:D, :], ACT.Copy).then_inc(s["prep_high"], 1)

            def gelu0(g, banks):
                wait(act, s["w2_done"], g)
                for j in range(HJ):
                    act.wait_ge(s["hid_psum"], 3 * g + j + 1)
                    act.activation(hid[:, j * TILE:(j + 1) * TILE], bank[banks[j]][:, :], ACT.Gelu,
                                   bias=B[f"b1_{j}"]).then_inc(s["gelu_done"], 1)

            def split3(f):
                if tile_known(f):
                    act.wait_ge(s["tr3_done"], f + 1)
                    wait(act, s["x3_lo"], f)
                    wait(act, s["ugv_psum"], 3 * f)
                    split_high(xc3[0:D, :], xh3[0:D, :], bank[T_BANK][0:D, :], s["x3_split"])

            def normalize1(n):
                if not tile_known(n):
                    return
                act.wait_ge(s["ln1_step"], 4 * n + 4)
                act.wait_ge(s["x_loaded"], 16 * n + 16)
                wait(act, s["trx_done"], n)
                xt = x_tile(n)
                for k in range(CHUNKS):
                    act.activation(xn1[:, k * D:(k + 1) * D], xt[:, k * D:(k + 1) * D], ACT.Identity,
                                   bias=ng1[:, k:k + 1], scale=rs1[:, k:k + 1]).then_inc(s["xn1_ready"], 1)

            def padded_images(f):
                if not tile_known(f):
                    return
                act.wait_ge(s["p_psum"], 2 * f + 2)
                if peeled(f, 0):
                    act.wait_ge(s["pads_zero"], 4)
                    act.wait_ge(s["prep"], PREP_BIAS0)
                padded = (pA[:, LEAD:LEAD + 2 * IMG].rearrange("c (i r w) -> c i r w", i=2, w=ROW),
                          pB[:, LEAD:LEAD + IMG].rearrange("c (i r w) -> c i r w", i=1, w=ROW))
                for grp, psum in enumerate((bank[2][:, :], bank[3][:, 0:TOKENS])):
                    wait(act, s["conv_step"], 16 * f + grp - 1)
                    act.activation(padded[grp][:, :, 0:SIDE, 0:SIDE],
                                   psum.rearrange("c (i r w) -> c i r w", r=SIDE, w=SIDE),
                                   ACT.Identity, bias=B[("inA", "inB")[grp]]).then_inc(s["p_ready"], 1)
                for grp, (acc, src) in enumerate(tap_views(0)):
                    wait(act, s["cT_done"], 2 * f + grp - 1)
                    act.wait_ge(s["p_ready"], 2 * f + 1 + grp)
                    act.activation(acc, src, ACT.Copy, scale=col(("kA0", "kB0")[grp]))\
                       .then_inc(s["tap0_done"], 1)

            def body0(i):
                n, f, m, g = i + 2, i + 1, i - 1, i - 2
                if tile_known(m):
                    for k in range(2):
                        if k == 0:
                            act.wait_ge(s["cT_done"], 2 * m + 2)
                            wait(act, s["mix_done"], 2 * m)
                        act.activation(local[:, k * 384:(k + 1) * 384], bank[4 + k][:, 0:384],
                                       ACT.Copy).then_inc(s["local_ready"], 1)
                if peeled(i, TILES):
                    split3(0)
                if tile_known(f):
                    act.wait_ge(s["trx_done"], f + 1)
                    wait(act, s["x1_lo"], f)
                    wait(act, s["p_psum"], 2 * f)
                    split_high(xc1[0:D, :].rearrange("c (i p a) -> c i a p", i=2, a=2),
                               xh1[0:D, :].rearrange("c (i p a) -> c i a p", i=2, a=2),
                               bank[0][0:D, :].rearrange("c (i a p) -> c i a p", i=2, a=2), s["x1_split"])
                if tile_known(m):
                    wait(act, s["mtr_done"], m)
                    wait(act, s["mvm_ready"], 4 * m)
                    for a in range(2):
                        act.wait_ge(s["mix_done"], 2 * m + a + 1)
                        act.activation(mixed[:, a * 384:(a + 1) * 384], bank[4 + a][:, 0:384],
                                       ACT.Copy).then_inc(s["mixed_ready"], 1)
                if tile_known(g):
                    act.wait_ge(s["tr2_done"], g + 1)
                    wait(act, s["x2_lo"], g)
                    wait(act, s["hid_psum"], 3 * g)
                    split_high(xc2[0:D, :], xh2[0:D, :], bank[1][0:D, :], s["x2_split"])
                if tile_known(m):
                    act.wait_ge(s["mtr_done"], m + 1)
                    wait(act, s["wout_done"], m)
                    act.activation(mcA[:, :], bank[4][:, :], ACT.Copy).then_inc(s["mc_ready"], 1)
                    act.activation(mcB[:, :], bank[5][:, 0:TOKENS], ACT.Copy).then_inc(s["mc_ready"], 1)
                first_w_in = peeled(i, -1)
                if first_w_in:
                    padded_images(f)
                else:
                    normalize1(n)
                if peeled(i, 1):
                    setup2()
                if peeled(i, TILES):
                    evac_ugv(0)
                    for k in range(2):
                        act.wait_ge(s["bits_set"], 2 * k + 2)
                        seed(0, k)
                if tile_known(g) and not is_last(g):
                    gelu0(g, (6, 7, 6))
                if not first_w_in:
                    padded_images(f)
                else:
                    normalize1(n)

            def evac_ugv(c):
                v_bank, g_bank, u_bank = vgu_bank(c)
                act.wait_ge(s["ugv_psum"], 3 * c + 1)
                wait(act, s["seeded"], SEEDS * c)
                act.activation(vh[0:D, :], bank[v_bank][0:D, :], ACT.Identity,
                               bias=B["v_half"][0:D]).then_inc(s["ugv_ready"], 1)
                act.wait_ge(s["ugv_psum"], 3 * c + 2)
                wait(act, s["q_ready"], QS * c)
                act.activation(th[0:D, :], bank[g_bank][0:D, :], ACT.Tanh, bias=B["g_half"][0:D],
                               scale=0.5).then_inc(s["ugv_ready"], 1)
                act.wait_ge(s["ugv_psum"], 3 * c + 3)
                wait(act, s["h8_ready"], c)
                act.activation(nu[0:D, :], bank[u_bank][0:D, :], ACT.Identity, bias=B["u_neg_half"][0:D],
                               scale=-0.5).then_inc(s["ugv_ready"], 1)
                act.wait_ge(s["ugv_ready"], 3 * c + 1)

            def seed(c, k):
                if tile_known(c):
                    for h in range(2):
                        if k != 1:
                            wait(act, s["q_ready"], QS * c + (2 * k - 2 + h if k else h - 1))
                        act.activation(rec(k, h), vh[0:D, half(h)], ACT.Copy).then_inc(s["seeded"], 1)

            def turn():
                seed(0, 2)
                seed(0, 3)
                body0(TILES + 1)
                seed(0, 4)
                split3(1)
                seed(0, 5)
                seed(0, 6)
                gelu0(TILES - 1, M1_BANK)
                act.preload_act_table(ACT.Gelu_apprx_tanh)

            def body1(i):
                f, c, m, g = i + 1, i, i - 1, i - 2

                def gelu(j):
                    if tile_known(g):
                        if j == 0:
                            wait(act, s["m2_done"], g)
                        act.wait_ge(s["hid1_psum"], 3 * g + j + 1)
                        act.activation(hid1[:, j * TILE:(j + 1) * TILE], bank[M1_BANK[j]][:, :],
                                       ACT.Gelu_apprx_tanh, bias=B[f"m1_{j}"]).then_inc(s["gelu1_done"], 1)

                if tile_known(c):
                    evac_ugv(c)
                seed(c, 0)
                seed(c, 1)
                gelu(0)
                gelu(1)
                seed(c, 2)
                gelu(2)
                seed(c, 3)
                split3(f)
                seed(c, 4)
                seed(c, 5)
                seed(c, 6)
                if tile_known(m):
                    act.wait_ge(s["tr4_done"], m + 1)
                    wait(act, s["x4_lo"], m)
                    wait(act, s["hid1_psum"], 3 * m)
                    split_high(xc4[0:D, :], xh4[0:D, :], bank[T_BANK][0:D, :], s["x4_split"])

            act.preload_act_table(ACT.Gelu)
            run(act, body0, body1, turn)

        @block.vector
        def _(dve):
            def stats(st, mv, chunk, step, ready, t, between):
                for k in range(CHUNKS):
                    dve.bn_stats(st[:, 6 * k:6 * k + 6], chunk(k)).then_inc(step, 1)
                between(0)
                dve.wait_ge(step, 4 * t + 4)
                between(1)
                for k in range(CHUNKS):
                    dve.bn_aggr(mv[:, 2 * k:2 * k + 2], st[:, 6 * k:6 * k + 6]).then_inc(ready, 1)

            count = [0]

            def prep(instruction):
                count[0] += 1
                instruction.then_inc(s["prep"], 1)
                return count[0]

            def split_weight(v, hi, lo, width, done):
                dve.wait_ge(s["prep"], done)
                high = prep(dve.tensor_copy(hi[0:D, 0:width], v[0:D, 0:width]))
                dve.wait_ge(s["prep"], high)
                return prep(dve.tensor_tensor(lo[0:D, 0:width], v[0:D, 0:width],
                                              hi[0:D, 0:width].bitcast(F32), ALU.subtract))

            def w0s(name, n=P):
                return w0[0:n, W0[name][0]:W0[name][1]]

            def w1s(name, n=P):
                return w1[0:n, W1[name][0]:W1[name][1]]

            def scaled(res, v, factor):
                return prep(dve.tensor_scalar(res, v, factor, None, ALU.mult, ALU.bypass))

            def setup_w_in():
                dve.wait_ge(s["cols_loaded"], 16)
                dve.wait_ge(s["w0_loaded"], 16)
                done = scaled(wi_f[0:D, :], w0s("w_in", D), col("n1_g", D))
                done = split_weight(wi_f, wi_h, wi_l, 384, done)
                assert done == PREP_WIN

            def setup0():
                dve.wait_ge(s["ones_set"], 1)
                scaled(onbA[:, :], ones[:, :], col("on_bA"))
                scaled(onbB[:, :], ones[:, :], col("on_bB"))
                scaled(woA_f[:, :], w0s("w_outA"), col("on_gA"))
                done = scaled(woB_f[:, :], w0s("w_outB"), col("on_gB"))
                assert done == PREP_WOUT
                dve.wait_ge(s["prep_psum"], 1)
                for k, name in enumerate(("inA", "inB", "b1_0", "b1_1", "b1_2")):
                    done = prep(dve.tensor_tensor(B[name], bank[4][:, k:k + 1],
                                                  col({"inA": "b_inA", "inB": "b_inB"}.get(name, name)), ALU.add))
                assert done == PREP_BIAS0
                dve.wait_ge(s["prep_psum"], 2)
                dve.wait_ge(s["rows_loaded"], 16)
                done = prep(dve.tensor_tensor(brow[:, :], bank[5][:, 0:D], rows[:, 0:D], ALU.add))
                assert done == PREP_BROW
                dve.wait_ge(s["prep_psum"], 3)
                dve.wait_ge(s["pads_zero"], 4)
                for res, v, lo, hi in ((woA, woA_f, 0, P), (woB0, woB_f, 0, HB), (woB1, woB_f, HB, P)):
                    done = prep(dve.scalar_tensor_tensor(out=res[lo:hi, :], in0=bank[6][lo:hi, 0:D],
                                                         scalar=-1.0 / INNER, in1=v[lo:hi, :],
                                                         op0=ALU.mult, op1=ALU.add))
                assert done == PREP_WOC
                done = scaled(w1_f[0:D, :], w0s("w1", D), col("n2_g", D))
                done = split_weight(w1_f, w1_h, w1_l, 384, done)
                assert done == PREP_W1

            def setup1():
                dve.wait_ge(s["w1_loaded"], 16)
                prep(dve.tensor_tensor(a_i[0:D, :], w1s("A", D), ident[0:D, 0:D], ALU.subtract))
                done = scaled(a_half[0:D, :], w1s("A", D), 0.5)
                dve.wait_ge(s["prep_psum"], 4)
                done = prep(dve.tensor_copy(wuT[0:D, :], bank[7][0:D, 0:D]))
                assert done == PREP_WUT
                dve.wait_ge(s["prep_psum"], 5)
                bu = prep(dve.tensor_tensor(B["u"][0:D], bank[6][0:D, 0:1], col("bu", D), ALU.add))
                assert bu == PREP_BU
                prep(dve.tensor_tensor(B["g"][0:D], bank[6][0:D, 1:2], col("bg", D), ALU.add))
                for j in range(HJ):
                    done = prep(dve.tensor_tensor(B[f"m1_{j}"], bank[6][:, 2 + j:3 + j], col(f"m1_{j}"),
                                                  ALU.add))
                assert done == PREP_ALL

            def residual3(e, psum):
                dve.wait_ge(s["x2b_ready"], e + 1)
                dve.wait_ge(s["w2_done"], e + 1)
                dve.tensor_tensor(x_tile(e), psum[:, 0:384], x_tile(e), ALU.add).then_inc(s["x3_ready"], 1)

            def normalize(xn, v, mv, rs, ready):
                for k in range(CHUNKS):
                    dve.tensor_scalar(xn[:, k * D:(k + 1) * D], v[:, k * D:(k + 1) * D],
                                      mv[:, 2 * k:2 * k + 1], rs[:, k:k + 1],
                                      ALU.subtract, ALU.mult).then_inc(ready, 1)

            def ln3_stats(n, between=lambda h: None):
                dve.wait_ge(s["x3_ready"], n + 1)
                wait(dve, s["ln3_step"], 2 * n)
                wait(dve, s["xn3_ready"], 4 * n)
                xt = x_tile(n)
                stats(st3, mv3, lambda k: xt[:, k * D:(k + 1) * D], s["bn3_step"], s["mv3_ready"], n, between)

            def ln3_normalize(n):
                if tile_known(n):
                    dve.wait_ge(s["ln3_step"], 2 * n + 2)
                    wait(dve, s["tr3_done"], n)
                    normalize(xn3, x_tile(n), mv3, rs3, s["xn3_ready"])

            def head(i):
                if i == TILES - 2:
                    ln3_stats(0)
                if i == TILES - 1:
                    ln3_normalize(0)
                    ln3_stats(1)

            def body0(i):
                n, c, m, e = i + 2, i, i - 1, i - 3

                def tap(k, groups=(0, 1)):
                    if not tile_known(c):
                        return
                    for grp in groups:
                        acc, src = tap_views(k)[grp]
                        if k == 1:
                            dve.wait_ge(s["tap0_done"], 2 * c + 1 + grp)
                        else:
                            dve.wait_ge(s["conv_step"], 16 * c + 2 * k - 3 + grp)
                        dve.scalar_tensor_tensor(out=acc, in0=src, scalar=col(f"k{'AB'[grp]}{k}"), in1=acc,
                                                 op0=ALU.mult, op1=ALU.add).then_inc(s["conv_step"], 1)

                if peeled(i, -1):
                    setup_w_in()
                if tile_known(n):
                    dve.wait_ge(s["x_loaded"], 16 * n + 16)
                    wait(dve, s["ln1_step"], 4 * n)
                    xt = x_tile(n)
                    stats(st1, mv1, lambda k: xt[:, k * D:(k + 1) * D], s["bn1_step"], s["mv1_ready"], n,
                          between=lambda grp: tap(1, [grp]))
                else:
                    tap(1)
                if peeled(i, -1):
                    setup0()
                tap(2)
                tap(3)
                if tile_known(e):
                    residual3(e, bank[7])
                if peeled(i, 1):
                    setup1()
                tap(4)
                if tile_known(m):
                    dve.wait_ge(s["mixed_ready"], 2 * m + 2)
                    wait(dve, s["lnm_step"], 2 * m)

                    def chunk(k):
                        at = (k % 2) * 2 * INNER + (k // 2) * INNER
                        return mixed[:, at:at + INNER]

                    stats(stm, mvm, chunk, s["bnm_step"], s["mvm_ready"], m,
                          between=lambda grp: tap(5, [grp]))
                else:
                    tap(5)
                tap(6)
                tap(7)
                if peeled(i, TILES):
                    ln3_normalize(1)
                if tile_known(m):
                    dve.wait_ge(s["xb_ready"], m + 1)
                    dve.wait_ge(s["lnm_step"], 2 * m + 2)
                    wait(dve, s["xn2_ready"], 4 * m)
                    wait(dve, s["x2b_ready"], m)
                    dve.wait_ge(s["wout_done"], m + 1)
                    for k in range(CHUNKS):
                        dve.scalar_tensor_tensor(out=x2[:, k * D:(k + 1) * D], in0=bank[1][:, k * D:(k + 1) * D],
                                                 scalar=rsm[:, k:k + 1], in1=xb[:, k * D:(k + 1) * D],
                                                 op0=ALU.mult, op1=ALU.add).then_inc(s["x2_ready"], 1)
                    tap(8, [0])
                    wait(dve, s["ln2_step"], 3 * m)
                    dve.wait_ge(s["x2_ready"], 4 * m + 4)
                    stats(st2, mv2, lambda k: x2[:, k * D:(k + 1) * D], s["bn2_step"], s["mv2_ready"], m,
                          between=lambda grp: tap(8, [1]) if grp else None)
                else:
                    tap(8)

            def step(c, k, halves=(0, 1)):
                if tile_known(c):
                    for h in halves:
                        dve.wait_ge(s["step_done"], SEEDS * c + 2 * k + h + 1)
                        dve.scalar_tensor_tensor(out=q[0:D, half(h)], in0=th[0:D, half(h)], scalar=1.0,
                                                 in1=rec(k, h), op0=ALU.add, op1=ALU.mult)\
                           .then_inc(s["q_ready"], 1)

            def first_q(c):
                dve.wait_ge(s["ugv_ready"], 3 * c + 3)
                dve.scalar_tensor_tensor(out=q[0:D, :], in0=th[0:D, :], scalar=1.0, in1=nu[0:D, :],
                                         op0=ALU.add, op1=ALU.mult).then_inc(s["q_ready"], 1)

            def last_h(c):
                wait(dve, s["trh_done"], c)
                dve.wait_ge(s["q_ready"], QS * c + QS)
                dve.scalar_tensor_tensor(out=h8[0:D, :], in0=nu[0:D, :], scalar=-2.0, in1=q[0:D, :],
                                         op0=ALU.mult, op1=ALU.add).then_inc(s["h8_ready"], 1)

            def turn():
                first_q(0)
                for k in range(3):
                    step(0, k)
                residual3(TILES - 2, bank[7])
                step(0, 3)
                step(0, 4)
                ln3_stats(2, between=lambda h: step(0, 5, [h]))
                step(0, 6)
                last_h(0)
                residual3(TILES - 1, bank[T_BANK])
                ln3_normalize(2)

            def body1(i):
                n, c, m, g = i + 2, i, i - 1, i - 2
                if tile_known(c):
                    first_q(c)
                if tile_known(m):
                    dve.wait_ge(s["trh_done"], m + 1)
                    wait(dve, s["xn4_ready"], 4 * m)
                    wait(dve, s["x4b_ready"], m)
                    dve.tensor_tensor(x4[:, :], bank[T_BANK][:, 0:384], x_tile(m), ALU.add)\
                       .then_inc(s["x4_ready"], 1)
                    wait(dve, s["ln4_step"], 2 * m)
                    dve.wait_ge(s["x4_ready"], m + 1)
                    stats(st4, mv4, lambda k: x4[:, k * D:(k + 1) * D], s["bn4_step"], s["mv4_ready"], m,
                          between=lambda h: step(c, 0, [h]))
                else:
                    step(c, 0)
                step(c, 1)
                if tile_known(n):
                    ln3_stats(n, between=lambda h: step(c, 2, [h]))
                else:
                    step(c, 2)
                step(c, 3)
                if tile_known(m):
                    dve.wait_ge(s["ln4_step"], 2 * m + 2)
                    wait(dve, s["tr4_done"], m)
                    normalize(xn4, x4, mv4, rs4, s["xn4_ready"])
                step(c, 4)
                if is_last(m):
                    dve.wait_ge(s["x4_split"], 2 * m + 2)
                    dve.wait_ge(s["hid1_psum"], 3 * m)
                    dve.tensor_tensor(xl4[0:D, :], xc4[0:D, :], xh4[0:D, :].bitcast(F32), ALU.subtract)\
                       .then_inc(s["x4_lo"], 1)
                if tile_known(g):
                    dve.wait_ge(s["x4b_ready"], g + 1)
                    wait(dve, s["y_stored"], 16 * g)
                    dve.wait_ge(s["m2_done"], g + 1)
                    dve.tensor_tensor(y[:, :], bank[V_BANK][:, 0:384], x4b[:, :], ALU.add)\
                       .then_inc(s["y_ready"], 1)
                step(c, 5)
                ln3_normalize(n)
                step(c, 6)
                if tile_known(c):
                    last_h(c)

            run(dve, body0, body1, turn, head)

        @block.tensor
        def _(pe):
            def wc0(name, lo=0, hi=None, n=P):
                a, b = W0[name]
                return w0[0:n, a + lo:b if hi is None else a + hi]

            def wc1(name, lo=0, hi=None, n=P):
                a, b = W1[name]
                return w1[0:n, a + lo:b if hi is None else a + hi]

            def setup_bias():
                pe.wait_ge(s["cols_loaded"], 16)
                pe.wait_ge(s["w0_loaded"], 16)
                pe.matmul(bank[4][:, 0:1], wc0("w_in", 0, 128, D), col("n1_b", D), start=True, stop=True)
                pe.matmul(bank[4][:, 1:2], wc0("w_in", 128, 256, D), col("n1_b", D), start=True, stop=False)
                pe.matmul(bank[4][:, 1:2], wc0("w_in", 256, 384, D), col("n1_b", D), start=False, stop=True)
                pe.wait_ge(s["w0_rest_loaded"], 16)
                for j in range(HJ):
                    last = pe.matmul(bank[4][:, 2 + j:3 + j], wc0("w1", j * P, (j + 1) * P, D), col("n2_b", D),
                                     start=True, stop=True)
                last.then_inc(s["prep_psum"], 1)

            def setup_w_out():
                pe.wait_ge(s["prep"], PREP_WOUT)
                pe.matmul(bank[5][:, 0:D], onbA[:, :], wc0("w_outA"), start=True, stop=False)
                pe.matmul(bank[5][:, 0:D], onbB[0:HB, :], wc0("w_outB", n=HB), start=False, stop=True)\
                  .then_inc(s["prep_psum"], 1)
                pe.matmul(bank[6][:, 0:D], ones[:, :], woA_f[:, :], start=True, stop=False)
                pe.matmul(bank[6][:, 0:D], ones[0:HB, :], woB_f[0:HB, :], start=False, stop=True)\
                  .then_inc(s["prep_psum"], 1)

            def setup1():
                pe.wait_ge(s["w1_loaded"], 16)
                pe.transpose(bank[7][0:D, 0:D], wc1("Wu", n=D), ident[0:D, 0:D]).then_inc(s["prep_psum"], 1)
                pe.matmul(bank[6][0:D, 0:1], wc1("Wu", n=D), col("c3", D), start=True, stop=True)
                pe.matmul(bank[6][0:D, 1:2], wc1("Wg", n=D), col("c3", D), start=True, stop=True)
                for j in range(HJ):
                    last = pe.matmul(bank[6][:, 2 + j:3 + j], wc1("m1", j * P, (j + 1) * P, D), col("c4", D),
                                     start=True, stop=True)
                last.then_inc(s["prep_psum"], 1)

            def setup2():
                pe.wait_ge(s["prep"], PREP_BU)
                pe.matmul(bank[7][0:D, P:P + D], wuT[0:D, :], a_i[0:D, :], start=True, stop=True)
                pe.matmul(bank[7][0:D, 2 * P:2 * P + 1], a_i[0:D, :], B["u"][0:D], start=True, stop=True)\
                  .then_inc(s["prep_psum"], 1)

            def transposes(dst, src, done):
                for k in range(CHUNKS):
                    last = pe.transpose(dst[0:D, k * P:(k + 1) * P], src[:, k * D:(k + 1) * D], ident[:, :])
                last.then_inc(done, 1)

            def three_passes(dst, wh, wl, xh, xl, first=True, last=True):
                pe.matmul(dst, wh, xh, start=first, stop=False)
                pe.matmul(dst, wh, xl, start=False, stop=False)
                return pe.matmul(dst, wl, xh, start=False, stop=last)

            def mlp1(g, j, psum):
                if j == 0:
                    pe.wait_ge(s["x2_lo"], g + 1)
                    pe.wait_ge(s["x2_split"], 2 * g + 2)
                    wait(pe, s["gelu_done"], 3 * g)
                w = slice(P * j, P * (j + 1))
                three_passes(psum[:, :], w1_h[0:D, w], w1_l[0:D, w], xh2[0:D, :], xl2[0:D, :])\
                    .then_inc(s["hid_psum"], 1)

            def mlp2(e, j, psum):
                pe.wait_ge(s["gelu_done"], 3 * e + max(j + 1, 2))
                for k in range(CHUNKS):
                    last = pe.matmul(psum[:, k * D:(k + 1) * D],
                                     hid[:, j * TILE + k * P:j * TILE + (k + 1) * P],
                                     wc0("w2", j * D, (j + 1) * D), start=(j == 0 and k == 0),
                                     stop=(j == HJ - 1), skip_group_check=True)
                if j == HJ - 1:
                    last.then_inc(s["w2_done"], 1)

            def ln3_transposes(f):
                pe.wait_ge(s["xn3_ready"], 4 * f + 4)
                if peeled(f, 1):
                    pe.wait_ge(s["ugv_ready"], 3)
                else:
                    wait(pe, s["x4_ready"], f - 1)
                transposes(bank[T_BANK], xn3, s["tr3_done"])

            def ugv(f, k):
                if k == 0:
                    pe.wait_ge(s["x3_lo"], f + 1)
                    pe.wait_ge(s["x3_split"], 2 * f + 2)
                    if peeled(f, 0):
                        pe.wait_ge(s["p_ready"], 2 * TILES)
                    else:
                        wait(pe, s["y_ready"], f - 2)
                w = slice((2, 1, 0)[k] * D, ((2, 1, 0)[k] + 1) * D)
                three_passes(bank[vgu_bank(f)[k]][0:D, :], w3_h[0:D, w], w3_l[0:D, w],
                             xh3[0:D, :], xl3[0:D, :]).then_inc(s["ugv_psum"], 1)

            def ln2_transposes(g):
                pe.wait_ge(s["xn2_ready"], 4 * g + 4)
                pe.wait_ge(s["x2_ready"], 4 * g + 4)
                transposes(bank[1], xn2, s["tr2_done"])

            def set_bits():
                for k in range(2):
                    if k == 0:
                        pe.wait_ge(s["mc_ready"], 2 * TILES)
                    else:
                        pe.wait_ge(s["ugv_ready"], 2)
                    for h in range(2):
                        pe.matmul(rec(k, h), a_half[0:D, :], xc1[0:D, half(h)], start=True, stop=True)\
                          .then_inc(s["bits_set"], 1)

            def rec_step(c, k):
                if tile_known(c):
                    for h in range(2):
                        pe.wait_ge(s["seeded"], SEEDS * c + 2 * k + h + 1)
                        pe.wait_ge(s["q_ready"], QS * c + max(2 * k + h, 1))
                        pe.matmul(rec(k, h), a_half[0:D, :], q[0:D, half(h)], start=False, stop=True,
                                  skip_group_check=True).then_inc(s["step_done"], 1)

            def body0(i):
                f, m, g, e = i + 1, i - 1, i - 2, i - 3
                if peeled(i, 1):
                    pe.wait_ge(s["prep"], PREP_WOC)
                if tile_known(e):
                    mlp2(e, 0, bank[7])
                if tile_known(m):
                    wait(pe, s["mc_ready"], 2 * m)
                    for grp, parts in enumerate((((0, cA, 0), (2, cA, 2 * P + SIDE)), ((1, cB, 0),))):
                        pe.wait_ge(s["conv_step"], 16 * m + 15 + grp)
                        for k in range(2):
                            for part, acc, at in parts:
                                last = pe.transpose(bank[4 + k][:, part * P:(part + 1) * P],
                                                    acc[:, at + k * P:at + (k + 1) * P], ident[:, :])
                        last.then_inc(s["cT_done"], 1)
                if peeled(i, -1):
                    setup_bias()
                if tile_known(f):
                    pe.wait_ge(s["xn1_ready"], 4 * f + 4)
                    wait(pe, s["x1_split"], 2 * f)
                    if peeled(i, -1):
                        pe.wait_ge(s["ident_loaded"], 16)
                    transposes(bank[0], xn1, s["trx_done"])
                if peeled(i, -1):
                    setup_w_out()
                if peeled(i, 1):
                    setup1()
                if tile_known(e):
                    mlp2(e, 1, bank[7])
                    mlp2(e, 2, bank[7])
                if peeled(i, TILES):
                    ln3_transposes(0)
                if tile_known(m):
                    pe.wait_ge(s["local_ready"], 2 * m + 2)
                    if peeled(i, 1):
                        pe.wait_ge(s["mix_loaded"], 16)
                    for a in range(2):
                        for k in range(2):
                            last = pe.matmul(bank[4 + a][:, 0:384],
                                             mix[:, k * TOKENS + a * P:k * TOKENS + (a + 1) * P],
                                             local[:, k * 384:(k + 1) * 384], start=(k == 0), stop=(k == 1))
                        last.then_inc(s["mix_done"], 1)
                if peeled(i, 1):
                    setup2()
                if tile_known(g):
                    ln2_transposes(g)
                if tile_known(m):
                    pe.wait_ge(s["mixed_ready"], 2 * m + 2)
                    for im in range(2):
                        for a in range(2):
                            src = mixed[:, a * 384 + 2 * P * im:a * 384 + 2 * P * im + P]
                            k = 2 * im + a
                            pe.transpose(bank[4][:, k * P:(k + 1) * P], src, ident[:, :])
                    for a in range(2):
                        last = pe.transpose(bank[5][:, a * P:(a + 1) * P], mixed[:, a * 384 + P:a * 384 + 2 * P],
                                            ident[:, :])
                    last.then_inc(s["mtr_done"], 1)
                if peeled(i, TILES):
                    for k in range(3):
                        ugv(0, k)
                if tile_known(f):
                    pe.wait_ge(s["x1_lo"], f + 1)
                    pe.wait_ge(s["x1_split"], 2 * f + 2)
                    if peeled(i, -1):
                        pe.wait_ge(s["prep"], PREP_WIN)
                    wait(pe, s["p_ready"], 2 * f)
                    three_passes(bank[2][:, :], wi_h[0:D, 0:P], wi_l[0:D, 0:P], xh1[0:D, :], xl1[0:D, :])\
                        .then_inc(s["p_psum"], 1)
                    for im in range(2):
                        w = slice(P * (im + 1), P * (im + 2))
                        x_ = slice(TOKENS * im, TOKENS * (im + 1))
                        last = three_passes(bank[3][:, 0:TOKENS], wi_h[0:D, w], wi_l[0:D, w], xh1[0:D, x_],
                                            xl1[0:D, x_], first=(im == 0), last=(im == 1))
                    last.then_inc(s["p_psum"], 1)
                if tile_known(m):
                    pe.wait_ge(s["mc_ready"], 2 * m + 2)
                    wait(pe, s["x2_split"], 2 * m)
                    for k in range(CHUNKS):
                        im, a = k // 2, k % 2
                        pe.matmul(bank[1][:, k * D:(k + 1) * D], mcA[:, k * P:(k + 1) * P], woA[:, :],
                                  start=True, stop=False)
                        last = pe.matmul(bank[1][:, k * D:(k + 1) * D], mcB[:, a * P:(a + 1) * P],
                                         (woB0, woB1)[im][:, :], start=False, stop=True)
                    last.then_inc(s["wout_done"], 1)
                if peeled(i, TILES):
                    set_bits()
                if tile_known(g) and not is_last(g):
                    if peeled(i, 2):
                        pe.wait_ge(s["prep"], PREP_ALL)
                        pe.wait_ge(s["prep_high"], 9)
                        pe.wait_ge(s["prep_low"], 2)
                    mlp1(g, 0, bank[6])
                    wait(pe, s["x3_ready"], g)
                    mlp1(g, 1, bank[7])
                    pe.wait_ge(s["gelu_done"], 3 * g + 1)
                    mlp1(g, 2, bank[6])

            def turn():
                last = TILES - 1
                rec_step(0, 0)
                mlp2(last - 1, 0, bank[7])
                rec_step(0, 1)
                mlp2(last - 1, 1, bank[7])
                rec_step(0, 2)
                mlp2(last - 1, 2, bank[7])
                ln2_transposes(last)
                rec_step(0, 3)
                ln3_transposes(1)
                rec_step(0, 4)
                mlp1(last, 0, bank[M1_BANK[0]])
                pe.wait_ge(s["x3_ready"], last)
                mlp1(last, 1, bank[M1_BANK[1]])
                rec_step(0, 5)
                mlp1(last, 2, bank[M1_BANK[2]])
                mlp2(last, 0, bank[T_BANK])
                rec_step(0, 6)
                mlp2(last, 1, bank[T_BANK])
                mlp2(last, 2, bank[T_BANK])
                for k in range(3):
                    ugv(1, k)

            def ln4_transposes(m):
                pe.wait_ge(s["xn4_ready"], 4 * m + 4)
                pe.wait_ge(s["x4_ready"], m + 1)
                if tile_known(m + 2):
                    pe.wait_ge(s["x3_split"], 2 * (m + 2) + 2)
                transposes(bank[T_BANK], xn4, s["tr4_done"])

            def body1(i):
                f, c, m, g = i + 1, i, i - 1, i - 2

                def m1(j):
                    if tile_known(g):
                        if j == 0:
                            pe.wait_ge(s["x4_lo"], g + 1)
                            pe.wait_ge(s["x4_split"], 2 * g + 2)
                        if tile_known(c):
                            pe.wait_ge(s["ugv_ready"], 3 * c + j + 1)
                        elif j == 0:
                            pe.wait_ge(s["y_ready"], g)
                        w = slice(P * j, P * (j + 1))
                        three_passes(bank[M1_BANK[j]][:, :], m1_h[0:D, w], m1_l[0:D, w],
                                     xh4[0:D, :], xl4[0:D, :]).then_inc(s["hid1_psum"], 1)

                def m2(j):
                    if tile_known(g):
                        pe.wait_ge(s["gelu1_done"], 3 * g + j + 1)
                        for k in range(CHUNKS):
                            last = pe.matmul(bank[V_BANK][:, k * D:(k + 1) * D],
                                             hid1[:, j * TILE + k * P:j * TILE + (k + 1) * P],
                                             wc1("m2", j * D, (j + 1) * D), start=(j == 0 and k == 0),
                                             stop=(j == HJ - 1), skip_group_check=True)
                        if j == HJ - 1:
                            last.then_inc(s["m2_done"], 1)

                if tile_known(m):
                    pe.wait_ge(s["h8_ready"], m + 1)
                    if peeled(m, 0):
                        pe.wait_ge(s["x3_ready"], TILES)
                    else:
                        pe.wait_ge(s["x4_split"], 2 * m)
                    for k in range(CHUNKS):
                        last = pe.transpose(bank[T_BANK][:, k * D:(k + 1) * D], h8[0:D, k * P:(k + 1) * P],
                                            ident[0:D, 0:D])
                    last.then_inc(s["trh_done"], 1)
                m1(0)
                m1(1)
                rec_step(c, 0)
                m1(2)
                rec_step(c, 1)
                if tile_known(f):
                    ln3_transposes(f)
                m2(0)
                rec_step(c, 2)
                m2(1)
                rec_step(c, 3)
                if is_last(m):
                    ln4_transposes(m)
                m2(2)
                rec_step(c, 4)
                if tile_known(m) and not is_last(m):
                    ln4_transposes(m)
                rec_step(c, 5)
                if tile_known(f):
                    ugv(f, 0)
                rec_step(c, 6)
                if tile_known(f):
                    ugv(f, 1)
                    ugv(f, 2)

            run(pe, body0, body1, turn)



VECTORS = {
    "n1_g": "L0_conv_n1_g", "n1_b": "L0_conv_n1_b", "n2_g": "L0_conv_n2_g", "n2_b": "L0_conv_n2_b",
    "s3": "L1_conv_norm1_scale", "c3": "L1_conv_norm1_bias", "bu": "L1_conv_bu", "bg": "L1_conv_bg",
    "s4": "L1_conv_norm2_scale", "c4": "L1_conv_norm2_bias"}


def kernel(**inputs):
    import numpy as np
    import concourse.bacc as bacc
    from concourse.bass_utils import run_bass_kernel_spmd

    a = {k: np.asarray(v) for k, v in inputs.items()}
    cols = np.zeros((P, len(COLS)), np.float32)

    def put(name, v):
        cols[:len(v), COLS.index(name)] = v

    def put_inner(name, v):
        put(name.replace("?", "A"), v[:P])
        put(name.replace("?", "B"), np.concatenate([v[P:], v[P:]]))

    for name, source in VECTORS.items():
        put(name, a[source])
    put_inner("b_in?", a["L0_conv_b_in"])
    put_inner("on_g?", a["L0_conv_on_g"])
    put_inner("on_b?", a["L0_conv_on_b"])
    taps = a["L0_conv_k_conv"].reshape(9, INNER)
    for t in range(9):
        put_inner(f"k?{t}", taps[t])
    for j in range(HJ):
        put(f"b1_{j}", a["L0_conv_b1"][j * P:(j + 1) * P])
        put(f"m1_{j}", a["L1_conv_mlp_b1"][j * P:(j + 1) * P])
    rows = np.concatenate([a["L0_conv_b_out"], a["L0_conv_b2"], a["L1_conv_mlp_b2"]])[None, :]

    w0 = np.zeros((P, 1248), np.float32)
    w0[:D, 0:P] = a["L0_conv_w_in"][:, :P]
    w0[:D, P:P + HB] = a["L0_conv_w_in"][:, P:]
    w0[:D, 2 * P + HB:3 * P] = a["L0_conv_w_in"][:, P:]
    w0[:, 384:480] = a["L0_conv_w_out"][:P]
    w0[:, 480:576] = np.concatenate([a["L0_conv_w_out"][P:]] * 2)
    w0[:D, 576:960] = a["L0_conv_w1"]
    w0[:, 960:1248] = a["L0_conv_w2"].reshape(HJ, P, D).transpose(1, 0, 2).reshape(P, HJ * D)
    w1 = np.zeros((P, 960), np.float32)
    w1[:D, 0:96] = a["L1_conv_Wu"]
    w1[:D, 96:192] = a["L1_conv_Wg"]
    w1[:D, 192:288] = a["L1_conv_A"]
    w1[:D, 288:672] = a["L1_conv_mlp_w1"]
    w1[:, 672:960] = a["L1_conv_mlp_w2"].reshape(HJ, P, D).transpose(1, 0, 2).reshape(P, HJ * D)

    at = np.arange(SIDE)
    both_ways = GAIN * DECAY ** np.abs(at[:, None] - at[None, :]) * (1 + (at[:, None] == at[None, :]))
    eye = np.eye(SIDE)
    mix = np.eye(TOKENS) + 0.25 * (np.kron(eye, both_ways) + np.kron(both_ways, eye))
    mix = mix.reshape(TOKENS, P, 2).transpose(0, 2, 1).reshape(TOKENS, TOKENS).astype(np.float32)

    arrays = {"x": np.ascontiguousarray(a["x"].reshape(IMAGES * P, 2 * D)), "cols": cols, "rows": rows, "w0": w0,
              "w1": w1, "mix": mix, "ident": np.eye(P, dtype=np.float32)}
    nc = bacc.Bacc("TRN2", target_bir_lowering=False, num_devices=1)
    args = [nc.dram_tensor(f"in_{n}", v.shape, F32, kind="ExternalInput").ap() for n, v in arrays.items()]
    out = nc.dram_tensor("out", (IMAGES * P, 2 * D), F32, kind="ExternalOutput").ap()
    build(nc, *args, out)
    r = run_bass_kernel_spmd(nc, [{f"in_{n}": v for n, v in arrays.items()}], core_ids=[0])
    return r.results[0]["out"].reshape(IMAGES, SIDE, SIDE, D)
```
